# Optimizing a Trainium2 kernel written in Bass

```python
import numpy as np
import jax
import jax.numpy as jnp

def _softmax(x, axis=-1):
    return jax.nn.softmax(x, axis=axis)

def _gelu(x):
    return jax.nn.gelu(x, approximate=True)

def _silu(x):
    return jax.nn.silu(x)

def _sigmoid(x):
    return jax.nn.sigmoid(x)

def _layernorm(x, axis=-1, eps=1e-05):
    m = jnp.mean(x, axis=axis, keepdims=True)
    v = jnp.var(x, axis=axis, keepdims=True)
    return (x - m) / jnp.sqrt(v + eps)

def _scatter_add(tgt, idx, src, axis=0):
    return tgt.at[idx].add(src)

def _segment_sum(src, seg, n):
    return jax.ops.segment_sum(src, seg, n)
kernel_name = 'mk_hybrid_d1_jaxref_r8_91c56b'

def setup_inputs(seed: int=0):
    np.random.seed(seed)
    _w = jnp.asarray

    def _L0_attn_a_setup():
        import jax, jax.numpy as jnp
        import numpy as np
        N_HEAD = 16
        N_LANDMARKS = 64
        N_ITER = 6

        def _landmarks(t, nL):
            B, nh, T, hs = t.shape
            return t.reshape(B, nh, nL, T // nL, hs).mean(axis=3)

        def _iterative_inv(K, n_iter=N_ITER):
            I = jnp.eye(K.shape[-1], dtype=K.dtype)
            denom = jnp.max(jnp.sum(K, axis=-2), axis=-1)[..., None, None]
            V = K.swapaxes(-1, -2) / denom
            for _ in range(n_iter):
                KV = K @ V
                V = 0.25 * V @ (13.0 * I - KV @ (15.0 * I - KV @ (7.0 * I - KV)))
            return V
        key = jax.random.key(seed)
        k1, k2, k3 = jax.random.split(key, 3)
        B, T, C = (4, 512, 128)
        x = jax.random.normal(k1, (B, T, C), dtype=jnp.float32)
        W_attn = jax.random.normal(k2, (C, 3 * C), dtype=jnp.float32) * (1.0 / np.sqrt(C))
        W_proj = jax.random.normal(k3, (C, C), dtype=jnp.float32) * (1.0 / np.sqrt(C))
        return {'x': x, 'W_attn': W_attn, 'W_proj': W_proj}
    _L0_attn_a_in = _L0_attn_a_setup()

    def _L0_attn_b_setup():
        import jax, jax.numpy as jnp
        import numpy as np
        D_CONV = 4
        DT_RANK = 64
        D_STATE = 16

        def _selective_scan(u, delta, A, Bm, Cm, D):
            b, l, d = u.shape
            n = A.shape[1]
            deltaA = jnp.exp(jnp.einsum('bld,dn->bldn', delta, A))
            dBu = delta[..., None] * Bm[:, :, None, :] * u[..., None]

            def step(state, inp):
                dA_t, dBu_t, C_t = inp
                state = dA_t * state + dBu_t
                y_t = jnp.einsum('bdn,bn->bd', state, C_t)
                return (state, y_t)
            init = jnp.zeros((b, d, n), u.dtype)
            xs = (jnp.swapaxes(deltaA, 0, 1), jnp.swapaxes(dBu, 0, 1), jnp.swapaxes(Cm, 0, 1))
            _, ys = jax.lax.scan(step, init, xs)
            y = jnp.swapaxes(ys, 0, 1)
            return y + u * D
        key = jax.random.key(seed)
        ks = jax.random.split(key, 10)
        d_model, d_in, L, B = (128, 256, 128, 2)
        s = 0.02
        x = jax.random.normal(ks[0], (B, L, d_model), jnp.float32)
        W_in = jax.random.normal(ks[1], (d_model, 2 * d_in), jnp.float32) * s
        conv_w = jax.random.normal(ks[2], (D_CONV, 1, d_in), jnp.float32) * s
        conv_b = jax.random.normal(ks[3], (d_in,), jnp.float32) * s
        W_x = jax.random.normal(ks[4], (d_in, DT_RANK + 2 * D_STATE), jnp.float32) * s
        W_dt = jax.random.normal(ks[5], (DT_RANK, d_in), jnp.float32) * s
        b_dt = jax.random.normal(ks[6], (d_in,), jnp.float32) * s
        A_log = jnp.log(jnp.tile(jnp.arange(1, D_STATE + 1, dtype=jnp.float32), (d_in, 1)))
        D = jnp.ones((d_in,), jnp.float32)
        W_out = jax.random.normal(ks[7], (d_in, d_model), jnp.float32) * s
        return {'x': x, 'W_in': W_in, 'conv_w': conv_w, 'conv_b': conv_b, 'W_x': W_x, 'W_dt': W_dt, 'b_dt': b_dt, 'A_log': A_log, 'D': D, 'W_out': W_out}
    _L0_attn_b_in = _L0_attn_b_setup()

    def _L0_ffn_setup():
        import jax, jax.numpy as jnp
        import numpy as np
        B, N, D = (4, 256, 128)
        SPARSITY = 0.01
        key = jax.random.key(seed)
        k1, k2, k3 = jax.random.split(key, 3)
        x = jax.random.normal(k1, (B, N, D), dtype=jnp.float32)
        spatial = jax.random.normal(k2, (D, D), dtype=jnp.float32) * 0.02
        freq = jnp.fft.fft(spatial, axis=-1)
        k = int(D * SPARSITY)
        mag = jnp.abs(freq)
        kth = jax.lax.top_k(mag, k)[0][:, -1:]
        w_sparse = jnp.where(mag >= kth, freq, 0.0 + 0j)
        bias = jax.random.normal(k3, (D,), dtype=jnp.float32) * 0.01
        return {'x': x, 'w_freq_real': jnp.real(w_sparse).astype(jnp.float32), 'w_freq_imag': jnp.imag(w_sparse).astype(jnp.float32), 'bias': bias}
    _L0_ffn_in = _L0_ffn_setup()
    _d = {'L0_attn_a_x': _L0_attn_a_in['x'], 'L0_attn_a_W_attn': _L0_attn_a_in['W_attn'], 'L0_attn_a_W_proj': _L0_attn_a_in['W_proj'], 'L0_attn_b_W_in': _L0_attn_b_in['W_in'], 'L0_attn_b_conv_w': _L0_attn_b_in['conv_w'], 'L0_attn_b_conv_b': _L0_attn_b_in['conv_b'], 'L0_attn_b_W_x': _L0_attn_b_in['W_x'], 'L0_attn_b_W_dt': _L0_attn_b_in['W_dt'], 'L0_attn_b_b_dt': _L0_attn_b_in['b_dt'], 'L0_attn_b_A_log': _L0_attn_b_in['A_log'], 'L0_attn_b_D': _L0_attn_b_in['D'], 'L0_attn_b_W_out': _L0_attn_b_in['W_out'], 'L0_ffn_w_freq_real': _L0_ffn_in['w_freq_real'], 'L0_ffn_w_freq_imag': _L0_ffn_in['w_freq_imag'], 'L0_ffn_bias': _L0_ffn_in['bias']}
    _x0 = _d['L0_attn_a_x']
    _d['L0_attn_a_x'] = jax.random.normal(jax.random.fold_in(jax.random.key(seed), 1), (16, 256, 128), dtype=_x0.dtype)
    del _x0
    return _d

def reference(L0_attn_a_x, L0_attn_a_W_attn, L0_attn_a_W_proj, L0_attn_b_W_in, L0_attn_b_conv_w, L0_attn_b_conv_b, L0_attn_b_W_x, L0_attn_b_W_dt, L0_attn_b_b_dt, L0_attn_b_A_log, L0_attn_b_D, L0_attn_b_W_out, L0_ffn_w_freq_real, L0_ffn_w_freq_imag, L0_ffn_bias):

    def _L0_attn_a_ref(x, W_attn, W_proj):
        import jax, jax.numpy as jnp
        import numpy as np
        N_HEAD = 16
        N_LANDMARKS = 64
        N_ITER = 6

        def _landmarks(t, nL):
            B, nh, T, hs = t.shape
            return t.reshape(B, nh, nL, T // nL, hs).mean(axis=3)

        def _iterative_inv(K, n_iter=N_ITER):
            I = jnp.eye(K.shape[-1], dtype=K.dtype)
            denom = jnp.max(jnp.sum(K, axis=-2), axis=-1)[..., None, None]
            V = K.swapaxes(-1, -2) / denom
            for _ in range(n_iter):
                KV = K @ V
                V = 0.25 * V @ (13.0 * I - KV @ (15.0 * I - KV @ (7.0 * I - KV)))
            return V
        B, T, C = x.shape
        nh, nL = (N_HEAD, N_LANDMARKS)
        hs = C // nh
        qkv = x @ W_attn
        q, k, v = jnp.split(qkv, 3, axis=-1)

        def heads(t):
            return t.reshape(B, T, nh, hs).transpose(0, 2, 1, 3)
        q, k, v = (heads(q), heads(k), heads(v))
        q_l = _landmarks(q, nL)
        k_l = _landmarks(k, nL)
        L = jax.nn.softmax(jnp.einsum('bhtd,bhld->bhtl', q, k_l), axis=-1)
        P = _iterative_inv(jax.nn.softmax(jnp.einsum('bhld,bhmd->bhlm', q_l, k_l), axis=-1))
        N = jax.nn.softmax(jnp.einsum('bhld,bhtd->bhlt', q_l, k), axis=-1)
        y = L @ (P @ (N @ v))
        y = y.transpose(0, 2, 1, 3).reshape(B, T, C)
        return y @ W_proj

    def _L0_attn_b_ref(x, W_in, conv_w, conv_b, W_x, W_dt, b_dt, A_log, D, W_out):
        import jax, jax.numpy as jnp
        import numpy as np
        D_CONV = 4
        DT_RANK = 64
        D_STATE = 16

        def _selective_scan(u, delta, A, Bm, Cm, D):
            b, l, d = u.shape
            n = A.shape[1]
            deltaA = jnp.exp(jnp.einsum('bld,dn->bldn', delta, A))
            dBu = delta[..., None] * Bm[:, :, None, :] * u[..., None]

            def step(state, inp):
                dA_t, dBu_t, C_t = inp
                state = dA_t * state + dBu_t
                y_t = jnp.einsum('bdn,bn->bd', state, C_t)
                return (state, y_t)
            init = jnp.zeros((b, d, n), u.dtype)
            xs = (jnp.swapaxes(deltaA, 0, 1), jnp.swapaxes(dBu, 0, 1), jnp.swapaxes(Cm, 0, 1))
            _, ys = jax.lax.scan(step, init, xs)
            y = jnp.swapaxes(ys, 0, 1)
            return y + u * D
        B, L, _ = x.shape
        d_in = W_in.shape[1] // 2
        x_and_res = x @ W_in
        x_, res = jnp.split(x_and_res, [d_in], axis=-1)
        x_pad = jnp.pad(x_, ((0, 0), (D_CONV - 1, 0), (0, 0)))
        x_conv = jax.lax.conv_general_dilated(x_pad, conv_w, window_strides=(1,), padding='VALID', dimension_numbers=('NWC', 'WIO', 'NWC'), feature_group_count=d_in)
        x_conv = x_conv[:, :L, :] + conv_b
        x_conv = jax.nn.silu(x_conv)
        A = -jnp.exp(A_log)
        x_dbl = x_conv @ W_x
        delta, Bm, Cm = jnp.split(x_dbl, [DT_RANK, DT_RANK + D_STATE], axis=-1)
        delta = jax.nn.softplus(delta @ W_dt + b_dt)
        y = _selective_scan(x_conv, delta, A, Bm, Cm, D)
        y = y * jax.nn.silu(res)
        return y @ W_out

    def _L0_ffn_ref(x, w_freq_real, w_freq_imag, bias):
        import jax, jax.numpy as jnp
        import numpy as np
        B, N, D = (4, 256, 128)
        SPARSITY = 0.01
        w = jax.lax.complex(w_freq_real, w_freq_imag)
        x_freq = jnp.fft.fft(x, axis=-1)
        y_freq = jnp.einsum('bnd,do->bno', x_freq, w)
        y = jnp.real(jnp.fft.ifft(y_freq, axis=-1))
        return y + bias
    x = L0_attn_a_x
    x = x + _L0_attn_a_ref(_layernorm(x, axis=-1), L0_attn_a_W_attn, L0_attn_a_W_proj)
    x = x + _L0_ffn_ref(_layernorm(x, axis=-1), L0_ffn_w_freq_real, L0_ffn_w_freq_imag, L0_ffn_bias)
    x = x + _L0_attn_b_ref(_layernorm(x, axis=-1), L0_attn_b_W_in, L0_attn_b_conv_w, L0_attn_b_conv_b, L0_attn_b_W_x, L0_attn_b_W_dt, L0_attn_b_b_dt, L0_attn_b_A_log, L0_attn_b_D, L0_attn_b_W_out)
    x = x + _L0_ffn_ref(_layernorm(x, axis=-1), L0_ffn_w_freq_real, L0_ffn_w_freq_imag, L0_ffn_bias)
    return x

_drawn_inputs = setup_inputs


def setup_inputs(seed=0):
    import zlib

    import numpy as np

    out = dict(_drawn_inputs(seed))
    spreads = {'L0_attn_b_D': (1.0, 0.6)}
    factors = {'L0_attn_b_W_in': 8.0,
     'L0_attn_b_conv_w': 8.0,
     'L0_attn_b_conv_b': 8.0,
     'L0_attn_b_W_x': 8.0,
     'L0_attn_b_W_dt': 8.0,
     'L0_attn_b_b_dt': 8.0,
     'L0_attn_b_A_log': 8.0,
     'L0_attn_b_W_out': 8.0,
     'L0_ffn_bias': 3.857}
    for name, (base, spread) in spreads.items():
        noise = np.random.default_rng([zlib.crc32(name.encode()), seed]).standard_normal(out[name].shape)
        drawn = base * np.exp(spread * noise) if base else spread * noise
        out[name] = jnp.asarray(drawn.astype(out[name].dtype))
    for name, factor in factors.items():
        out[name] = (out[name] * factor).astype(out[name].dtype)
    return out
```

```python
from contextlib import ExitStack

import numpy as np

import concourse.bass as bass
from concourse import mybir

F32 = mybir.dt.float32
BF16 = mybir.dt.bfloat16
ALU = mybir.AluOpType
ACT = mybir.ActivationFunctionType
AX = mybir.AxisListType

P = 128
B, T, C = 16, 256, 128
TT = T // P
NH, HS, NL = 16, 8, 64
NP = NH // 2
POOLED = T // NL
NITER = 6
ZC = NL + HS
VC = HS + 1
DI, DT = 256, 2
NS, RK, KC = 16, 64, 4
NQ = 4
NU = DT * NS // NQ
EPS = 1e-5
LN_MOST = 2.0 ** 62

TAB = {}
_at = 0
for _name, _n in (("ident", P), ("halfones", P), ("cos", P), ("sin", P), ("nsin", P), ("icos", P),
                  ("insin", P), ("headmask", 4), ("part1", 1), ("part2", 1), ("eps", 1), ("one", 1)):
    TAB[_name] = (_at, _at + _n)
    _at += _n
TABW = _at


def shape_tables():
    tab = np.zeros((P, TABW), np.float32)
    p = np.arange(P)
    angle = 2 * np.pi * (np.outer(p, p) % C) / C

    def put(name, a):
        tab[:, TAB[name][0]:TAB[name][1]] = a
    put("ident", np.eye(P))
    put("halfones", (p[:, None] // NL == p[None, :] // NL))
    put("cos", np.cos(angle))
    put("sin", np.sin(angle))
    put("nsin", -np.sin(angle))
    put("icos", np.cos(angle) / C)
    put("insin", -np.sin(angle) / C)
    put("headmask", (p[:, None] // HS % 4 == np.arange(4)[None, :]) / POOLED)
    put("part1", -(p[:, None] // NS >= 1).astype(np.float32))
    put("part2", -(p[:, None] // NS >= 2).astype(np.float32))
    put("eps", EPS)
    put("one", 1.0)
    pick = np.zeros((3 * NS, NS, P), np.float32)
    for r in range(3 * NS):
        pick[r, r % NS, :] = 1.0
    return tab, pick.reshape(3 * NS, NS * P)


class Link:

    def __init__(self, sem, per_batch):
        self.sem, self.per_batch = sem, per_batch

    def start(self, b):
        self.base, self.n = b * self.per_batch, 0

    def __call__(self, eng, ins):
        self.n += 1
        ins.then_inc(self.sem, 1)
        eng.wait_ge(self.sem, self.base + self.n)


def hybrid_layer_kernel(nc, x, W_attn, W_proj, W_in, conv_w, conv_b, W_x, W_dt, b_dt, A_log, D, W_out,
                        w_re, w_im, bias, tab, pick, out):
    ctx = ExitStack()
    with ctx:
        def sb(name, shape, dt=F32):
            return ctx.enter_context(nc.sbuf_tensor(name, shape, dt))

        def sem(name):
            return ctx.enter_context(nc.semaphore(name))

        tb = sb("tb", [P, TABW])
        pick_f = sb("pick_f", [3 * NS, NS * P])
        pick_s = sb("pick_s", [3 * NS, NS, P], BF16)
        wqkv = sb("wqkv", [P, 3 * C])
        wproj = sb("wproj", [P, C])
        win = sb("win", [P, 2 * DI])
        convw_b = sb("convw_b", [P, KC, DI])
        wconv = sb("wconv", [P, KC, DI])
        convb = sb("convb", [P, DT])
        nconvb = sb("nconvb", [P, DT])
        wx = sb("wx", [P, DT, RK + 2 * NS])
        wx3 = sb("wx3", [P, DT, 2, 3, NS])
        wdt = sb("wdt", [RK, DI])
        bdt = sb("bdt", [P, DT])
        negA = sb("negA", [P, DT, NS])
        dskip = sb("dskip", [P, DT])
        wout = sb("wout", [P, DT, C])
        wre = sb("wre", [P, P])
        wim = sb("wim", [P, P])
        fT = sb("fT", [P, 2, P])
        ffnM = sb("ffnM", [P, P])
        bias_b = sb("bias_b", [P, C])

        def const(name):
            return tb[:, TAB[name][0]:TAB[name][1]]
        ident = const("ident")

        xin = sb("xin", [P, TT, C])
        a_st = sb("a_st", [P, TT, 6])
        pause = sb("pause", [P, 1])
        a_mv = sb("a_mv", [P, TT, 2])
        a_rs = sb("a_rs", [P, 4, TT])
        a_xn = sb("a_xn", [P, TT, C])
        a_xT = sb("a_xT", [P, T])
        qkT = sb("qkT", [P, 2, T])
        v1 = sb("v1", [P, TT, NH, VC])
        lm = sb("lm", [P, 2, NL])
        qz = sb("qz", [P, 4, NL])
        kz = sb("kz", [P, 4, NL])
        klu = sb("klu", [P, NL])
        nmaxL = sb("nmaxL", [P, TT * NH])
        EL = sb("EL", [P, 4, TT, 4 * NL])
        ELT = sb("ELT", [P, TT, NP, P])
        nmaxN = sb("nmaxN", [P, NP])
        EN = sb("EN", [P, NP, T])
        ENT = sb("ENT", [P, TT, NP, P])
        nmaxK = sb("nmaxK", [P, NP])
        Ks = sb("Ks", [P, NP, NL])
        sumK = sb("sumK", [P, NP])
        rsumK = sb("rsumK", [P, NP])
        den = sb("den", [P, NP])
        rden = sb("rden", [P, NP])
        Kbd = sb("Kbd", [P, NP, P])
        rsumN = sb("rsumN", [P, NP])
        wv = sb("wv", [P, NP, HS])
        Yz = sb("Yz", [P, NP, ZC])
        Hz = sb("Hz", [P, NP, ZC])
        Mr = sb("Mr", [P, NP, ZC])
        Ybd = sb("Ybd", [P, NP, P])
        Abd = sb("Abd", [P, NP, P])
        zp = sb("zp", [P, NP, 2 * VC])
        rsumL = sb("rsumL", [P, TT * NH])
        yat = sb("yat", [P, TT, NH, HS])
        yT = sb("yT", [P, T])
        x1 = sb("x1", [P, TT, C])
        x1b = sb("x1b", [P, TT, C])
        x2 = sb("x2", [P, TT, C])

        m_st = sb("m_st", [P, TT, 6])
        m_mv = sb("m_mv", [P, TT, 2])
        m_rs = sb("m_rs", [P, 4, TT])
        m_xn = sb("m_xn", [P, TT, C])
        xpT = sb("xpT", [P, KC - 1 + T])
        f_xT = sb("f_xT", [P, T])
        gate = sb("gate", [P, 2, DT, T])
        u = sb("u", [P, DT, T])
        sres = sb("sres", [P, DT, T])
        dlr = sb("dlr", [RK, T])
        bc = sb("bc", [3 * NS, 2, T])
        bch = sb("bch", [3 * NS, 2, T], BF16)
        bcs = sb("bcs", [3 * NS, 2, T], BF16)
        spa = sb("spa", [P, DT, T])
        spp = sb("spp", [P, DT, T])
        delta = sb("delta", [P, DT, T])
        du = sb("du", [P, DT, T])
        c_sb = sb("c_sb", [P, NS, T])
        dA = sb("dA", [P, 2, NQ, T])
        dBu = sb("dBu", [P, 2, NQ, T])
        hst = sb("hst", [P, 2, NQ, T])
        hc = sb("hc", [P, 2, NQ, T])
        ym = sb("ym", [P, DT, T])
        x3 = sb("x3", [P, TT, C])
        x3b = sb("x3b", [P, TT, C])
        x4 = sb("x4", [P, TT, C])

        PA = ctx.enter_context(nc.psum_tensor("PA", [P, 4, 512], F32))
        PM = ctx.enter_context(nc.psum_tensor("PM", [P, 4, 512], F32))

        names = """weights_in tables_in x_in x_out
            pick_cast convw_ready nconvb_ready wx3_ready negA_ready zeros_ready fT_ps fT_sb ffnM_ps ffnM_sb
            a_var a_rs0 a_xn_ready a_xT_ps a_xT_ready qk_ps qk_ready v_ps v_ready lm_ready
            K_ps K_sub K_exp K_ready L_ps L_sub L_exp LT_ps LT_act LT_dve
            N_ps N_max N_exp NT_ps NT_act NT_dve Kbd_ready cy_ps nv_ps Y_ready w_ready z0_ps z_ready
            Ybd_ready sq_ps A_bd M_ready cube_ps YZ_ready zp_ready
            y_ps y_ready yT_ps yT_ready proj_ps x1_ready x1b_ready
            f1_var f1_rs0 f1_xn_ready f1_xT_ps f1_xT_ready f1_ps x2_ready
            m_var m_rs0 m_xn_ready m_xT_ps m_xT_ready in_ps gate_exp gate_cut gate_ready u_ready
            dbl_ps dlr_ready bc_hi bc_ready dt_ps abs_read sp_ready delta_ready du_ready
            b_ps c_ps c_ready dA_ready dBu_ready h_ready hc_ready y_acc ym_ready out_ps x3_ready x3b_ready
            f2_var f2_rs0 f2_xn_ready f2_xT_ps f2_xT_ready f2_ps x4_ready
            dve_a dve_m act_a act_m filled expA""".split()
        S = {n: sem(n) for n in names}
        NW = 15
        dve_a, dve_m = Link(S["dve_a"], 19), Link(S["dve_m"], 14)
        act_a, act_m = Link(S["act_a"], 2), Link(S["act_m"], 4)

        block = ctx.enter_context(nc.Block())

        @block.sync
        def _(sp):
            def load_x(b):
                sp.dma_start(xin[:, :, :], x[bass.ds(b, 1), :, :].rearrange("b (t p) c -> p (b t) c", p=P)
                             ).then_inc(S["x_in"], 16)

            def store(b):
                sp.wait_ge(S["x4_ready"], b + 1)
                sp.dma_start(out[bass.ds(b, 1), :, :].rearrange("b (t p) c -> p (b t) c", p=P), x4[:, :, :]
                             ).then_inc(S["x_out"], 16)

            sp.dma_start(tb[:, :], tab).then_inc(S["tables_in"], 16)
            load_x(0)
            sp.dma_start(pick_f[:, :], pick).then_inc(S["weights_in"], 16)
            sp.dma_start(wqkv[:, :], W_attn).then_inc(S["weights_in"], 16)
            sp.dma_start(wproj[:, :], W_proj).then_inc(S["weights_in"], 16)
            sp.dma_start(wre[:, :], w_re).then_inc(S["weights_in"], 16)
            sp.dma_start(wim[:, :], w_im).then_inc(S["weights_in"], 16)
            sp.dma_start(win[:, :], W_in).then_inc(S["weights_in"], 16)
            sp.dma_start(convw_b[:, :, :], conv_w.rearrange("k a d -> a k d").broadcast_to([P, KC, DI])
                         ).then_inc(S["weights_in"], 16)
            sp.dma_start(convb[:, :], conv_b.rearrange("(t p) -> p t", p=P),
                         allow_slow_non_contiguous=True).then_inc(S["weights_in"], 16)
            sp.dma_start(wx[:, :, :], W_x.rearrange("(t p) r -> p t r", p=P)).then_inc(S["weights_in"], 16)
            sp.dma_start(wdt[:, :], W_dt).then_inc(S["weights_in"], 16)
            sp.dma_start(bdt[:, :], b_dt.rearrange("(t p) -> p t", p=P),
                         allow_slow_non_contiguous=True).then_inc(S["weights_in"], 16)
            sp.dma_start(negA[:, :, :], A_log.rearrange("(t p) n -> p t n", p=P)).then_inc(S["weights_in"], 16)
            sp.dma_start(dskip[:, :], D.rearrange("(t p) -> p t", p=P),
                         allow_slow_non_contiguous=True).then_inc(S["weights_in"], 16)
            sp.dma_start(wout[:, :, :], W_out.rearrange("(t p) c -> p t c", p=P)).then_inc(S["weights_in"], 16)
            sp.dma_start(bias_b[:, :], bias.rearrange("(a c) -> a c", a=1).broadcast_to([P, C])
                         ).then_inc(S["weights_in"], 16)
            sp.wait_ge(S["x1_ready"], 1)
            load_x(1)
            store(0)
            with sp.Fori(2, B) as i:
                sp.wait_ge(S["x_out"], 16 * (i - 1))
                sp.wait_ge(S["x1_ready"], i)
                load_x(i)
                store(i - 1)
            store(B - 1)
            sp.wait_ge(S["x_out"], 16 * B)

        @block.tensor
        def _(pe):
            pe.wait_ge(S["tables_in"], 16)
            pe.wait_ge(S["weights_in"], 16 * NW)
            pe.matmul(PM[:, 0, 0:P], wre[:, :], const("cos"), start=True, stop=False)
            pe.matmul(PM[:, 0, 0:P], wim[:, :], const("sin"), start=False, stop=True)
            pe.matmul(PM[:, 0, P:2 * P], wim[:, :], const("cos"), start=True, stop=False)
            pe.matmul(PM[:, 0, P:2 * P], wre[:, :], const("nsin"), start=False, stop=True
                      ).then_inc(S["fT_ps"], 1)
            pe.wait_ge(S["fT_sb"], 1)
            pe.matmul(PM[:, 1, 0:P], fT[:, 0, :], const("icos"), start=True, stop=False)
            pe.matmul(PM[:, 1, 0:P], fT[:, 1, :], const("insin"), start=False, stop=True
                      ).then_inc(S["ffnM_ps"], 1)

            def turn(src, bank, done):
                for t in range(TT):
                    mm = pe.transpose(bank[:, t * P:(t + 1) * P], src[:, t, :], ident)
                mm.then_inc(done, 1)

            def front(b):
                pe.wait_ge(S["a_xn_ready"], b + 1)
                turn(a_xn, PA[:, 0, :], S["a_xT_ps"])
                pe.wait_ge(S["a_xT_ready"], b + 1)
                pe.matmul(PA[:, 1, 0:T], wqkv[:, 0:C], a_xT[:, :], start=True, stop=True)
                pe.matmul(PA[:, 1, T:2 * T], wqkv[:, C:2 * C], a_xT[:, :], start=True, stop=True
                          ).then_inc(S["qk_ps"], 1)
                for t in range(TT):
                    mm = pe.matmul(PA[:, 2, t * C:(t + 1) * C], a_xT[:, t * P:(t + 1) * P],
                                   wqkv[:, 2 * C:3 * C], start=True, stop=True)
                mm.then_inc(S["v_ps"], 1)

            def scores_L(b):
                pe.wait_ge(S["lm_ready"], b + 1)
                pe.wait_ge(S["v_ready"], b + 1)
                for t in range(TT):
                    for g in range(4):
                        mm = pe.matmul(PA[:, g, t * T:(t + 1) * T],
                                       qkT[32 * g:32 * g + 32, 0, t * P:(t + 1) * P],
                                       kz[32 * g:32 * g + 32, :, :], start=True, stop=True)
                mm.then_inc(S["L_ps"], 1)

            def scores_K(b):
                pe.wait_ge(S["LT_act"], b + 1)
                pe.wait_ge(S["LT_dve"], b + 1)
                for jp in range(2):
                    for g in range(4):
                        mm = pe.matmul(PA[:, g, jp * NL:(jp + 1) * NL],
                                       qz[32 * g:32 * g + 32, 2 * jp:2 * jp + 2, :],
                                       klu[32 * g:32 * g + 32, :], start=True, stop=True)
                mm.then_inc(S["K_ps"], 1)

            def scores_N(b):
                pe.wait_ge(S["K_sub"], b + 1)
                for jp in range(2):
                    for g in range(4):
                        mm = pe.matmul(PA[:, g, jp * T:(jp + 1) * T],
                                       qz[32 * g:32 * g + 32, 2 * jp:2 * jp + 2, :],
                                       qkT[32 * g:32 * g + 32, 1, :], start=True, stop=True)
                mm.then_inc(S["N_ps"], 1)

            def turn_L(b):
                pe.wait_ge(S["L_exp"], b + 1)
                for t in range(TT):
                    for p in range(NP):
                        mm = pe.transpose(PA[:, 2 * t + p // 4, p % 4 * P:(p % 4 + 1) * P],
                                          EL[:, p // 2, t, p % 2 * P:(p % 2 + 1) * P], ident)
                    mm.then_inc(S["LT_ps"], 1)

            def turn_N(b):
                pe.wait_ge(S["N_exp"], b + 1)
                for t in range(TT):
                    for p in range(NP):
                        mm = pe.transpose(PA[:, 2 * t + p // 4, p % 4 * P:(p % 4 + 1) * P],
                                          EN[:, p, t * P:(t + 1) * P], ident)
                    mm.then_inc(S["NT_ps"], 1)

            def inverse_start(b):
                pe.wait_ge(S["Kbd_ready"], b + 1)
                pe.wait_ge(S["NT_act"], b + 1)
                pe.matmul(PA[:, 0, :], const("halfones"), Ks[:, :, :], start=True, stop=True)
                for p in range(NP):
                    mm = pe.matmul(PA[:, 1, p * NL:(p + 1) * NL], Kbd[:, p, :], Ks[:, p, :],
                                   start=True, stop=True)
                mm.then_inc(S["cy_ps"], 1)
                pe.wait_ge(S["NT_dve"], b + 1)
                for p in range(NP):
                    for t in range(TT):
                        mm = pe.matmul(PA[:, 2, p * 2 * VC:(p + 1) * 2 * VC], ENT[:, t, p, :],
                                       v1[:, t, 2 * p:2 * p + 2, :], start=(t == 0), stop=(t == TT - 1))
                mm.then_inc(S["nv_ps"], 1)
                pe.wait_ge(S["w_ready"], b + 1)
                for p in range(NP):
                    mm = pe.matmul(PA[:, 3, p * HS:(p + 1) * HS], Kbd[:, p, :], wv[:, p, :],
                                   start=True, stop=True)
                mm.then_inc(S["z0_ps"], 1)

            def inverse_step(b, j):
                last = j == NITER - 1
                if j == 0:
                    pe.wait_ge(S["z_ready"], b + 1)
                for e in range(2):
                    pe.wait_ge(S["Ybd_ready"], b * 2 * NITER + 2 * j + e + 1)
                    for p in range(4):
                        q = 4 * e + p
                        mm = pe.matmul(PA[:, e, p * P:p * P + ZC], Ybd[:, q, :], Yz[:, q, :],
                                       start=True, stop=True)
                    mm.then_inc(S["sq_ps"], 1)
                for e in range(2):
                    pe.wait_ge(S["A_bd"], b * 2 * NITER + 2 * j + e + 1)
                    pe.wait_ge(S["M_ready"], b * 2 * NITER + 2 * j + e + 1)
                    c0 = NL if last else 0
                    for p in range(4):
                        q = 4 * e + p
                        mm = pe.matmul(PA[:, 2 + e, p * P + c0:p * P + ZC], Abd[:, q, :], Mr[:, q, c0:ZC],
                                       start=True, stop=True)
                    mm.then_inc(S["cube_ps"], 1)

            def attend(b):
                pe.wait_ge(S["zp_ready"], b + 1)
                for t in range(TT):
                    for p in range(NP):
                        at = (t * NP + p) * 2 * VC
                        mm = pe.matmul(PA[:, 0, at:at + 2 * VC], ELT[:, t, p, :], zp[:, p, :],
                                       start=True, stop=True)
                mm.then_inc(S["y_ps"], 1)
                pe.wait_ge(S["y_ready"], b + 1)
                turn(yat[:, :, :, :].rearrange("p t h d -> p t (h d)"), PA[:, 1, :], S["yT_ps"])
                pe.wait_ge(S["yT_ready"], b + 1)
                for t in range(TT):
                    mm = pe.matmul(PA[:, 2, t * C:(t + 1) * C], yT[:, t * P:(t + 1) * P], wproj[:, :],
                                   start=True, stop=True)
                mm.then_inc(S["proj_ps"], 1)

            def fourier(b, xn, bank_t, xT, bank_y, xn_ready, xT_ps, xT_ready, done):
                pe.wait_ge(xn_ready, b + 1)
                turn(xn, bank_t, xT_ps)
                pe.wait_ge(xT_ready, b + 1)
                for t in range(TT):
                    mm = pe.matmul(bank_y[:, t * C:(t + 1) * C], xT[:, t * P:(t + 1) * P], ffnM[:, :],
                                   start=True, stop=True)
                mm.then_inc(done, 1)

            def fourier1(b):
                fourier(b, a_xn, PA[:, 0, :], a_xT, PA[:, 1, :],
                        S["f1_xn_ready"], S["f1_xT_ps"], S["f1_xT_ready"], S["f1_ps"])

            def mamba_front(b):
                pe.wait_ge(S["m_xn_ready"], b + 1)
                turn(m_xn, PM[:, 0, :], S["m_xT_ps"])
                pe.wait_ge(S["m_xT_ready"], b + 1)
                for d in range(DT):
                    for k in range(KC):
                        pe.matmul(PM[:, 1, d * T:(d + 1) * T], wconv[:, k, d * P:(d + 1) * P],
                                  xpT[:, k:k + T], start=(k == 0), stop=(k == KC - 1))
                for d in range(DT):
                    mm = pe.matmul(PM[:, 2, d * T:(d + 1) * T], win[:, DI + d * P:DI + (d + 1) * P],
                                   xpT[:, KC - 1:KC - 1 + T], start=True, stop=True)
                mm.then_inc(S["in_ps"], 1)
                pe.wait_ge(S["u_ready"], b + 1)
                for d in range(DT):
                    pe.matmul(PM[0:RK, 0, 0:T], wx[:, d, 0:RK], u[:, d, :], start=(d == 0), stop=(d == DT - 1))
                for s in range(2):
                    for d in range(DT):
                        mm = pe.matmul(PM[0:3 * NS, 3, s * T:(s + 1) * T],
                                       wx3[:, d, s, :, :], u[:, d, :],
                                       start=(d == 0), stop=(d == DT - 1))
                mm.then_inc(S["dbl_ps"], 1)
                pe.wait_ge(S["dlr_ready"], b + 1)
                for d in range(DT):
                    mm = pe.matmul(PM[:, 1, d * T:(d + 1) * T], wdt[:, d * P:(d + 1) * P], dlr[:, :],
                                   start=True, stop=True)
                mm.then_inc(S["dt_ps"], 1)
                pe.wait_ge(S["bc_ready"], b + 1)
                pe.wait_ge(S["delta_ready"], b + 1)

            def spread_bc(b, q):
                if q > 0:
                    pe.wait_ge(S["dBu_ready"], b * NU + DT * q)
                for h in range(NQ // 2):
                    for n in range(2):
                        mm = pe.matmul(PM[:, h, n * T:(n + 1) * T], pick_s[:, NQ * q + 2 * h + n, :],
                                       bcs[:, 0, :], start=True, stop=True)
                mm.then_inc(S["b_ps"], 1)
                for h in range(NQ // 2):
                    if q > 0 or h > 0:
                        pe.wait_ge(S["c_ready"], b * NS // 2 + 2 * q + h)
                    for n in range(2):
                        mm = pe.matmul(PM[:, 2, n * T:(n + 1) * T], pick_s[:, NQ * q + 2 * h + n, :],
                                       bcs[:, 1, :], start=True, stop=True)
                    mm.then_inc(S["c_ps"], 1)

            def sum_states(b, k):
                d = k % DT
                pe.wait_ge(S["hc_ready"], b * NU + k + 1)
                for n in range(NQ):
                    mm = pe.matmul(PM[:, 3, d * T:(d + 1) * T], ident, hc[:, k % 2, n, :],
                                   start=(k == 0 and n == 0), stop=(k >= NU - DT and n == NQ - 1),
                                   skip_group_check=True)
                mm.then_inc(S["y_acc"], 1)

            def mamba_out(b):
                pe.wait_ge(S["ym_ready"], b + 1)
                for t in range(TT):
                    for d in range(DT):
                        mm = pe.matmul(PM[:, 0, t * C:(t + 1) * C], ym[:, d, t * P:(t + 1) * P],
                                       wout[:, d, :], start=(d == 0), stop=(d == DT - 1))
                mm.then_inc(S["out_ps"], 1)
                fourier(b, m_xn, PM[:, 1, :], f_xT, PM[:, 2, :],
                        S["f2_xn_ready"], S["f2_xT_ps"], S["f2_xT_ready"], S["f2_ps"])

            def attention(b, unit):
                front(b)
                scores_L(b)
                unit(0)
                turn_L(b)
                scores_K(b)
                scores_N(b)
                unit(1)
                turn_N(b)
                inverse_start(b)
                for j in range(NITER):
                    inverse_step(b, j)
                    unit(2 + j)

            def mamba_unit(b, k):
                if k % DT == 0:
                    spread_bc(b, k // DT)
                if k > 0:
                    sum_states(b, k - 1)

            pe.wait_ge(S["ffnM_sb"], 1)
            pe.wait_ge(S["pick_cast"], 1)
            pe.wait_ge(S["convw_ready"], 1)
            pe.wait_ge(S["wx3_ready"], 1)
            pe.wait_ge(S["zeros_ready"], 1)
            attention(0, lambda k: None)
            attend(0)
            fourier1(0)
            with pe.Fori(1, B) as i:
                mamba_front(i - 1)
                attention(i, lambda k: mamba_unit(i - 1, k))
                sum_states(i - 1, NU - 1)
                mamba_out(i - 1)
                attend(i)
                fourier1(i)
            mamba_front(B - 1)
            for k in range(NU):
                mamba_unit(B - 1, k)
            sum_states(B - 1, NU - 1)
            mamba_out(B - 1)

        @block.scalar
        def _(act):
            def copy(dst, src, scale=1.0):
                return act.activation(dst, src, ACT.Copy, scale=scale)

            def first_rstd(b, link, mv, rs, var, done):
                act.wait_ge(var, b + 1)
                link(act, act.activation(rs[:, 0, :], mv[:, :, 1], ACT.Ln, bias=const("eps")))
                act.activation(rs[:, 1, :], rs[:, 0, :], ACT.Exp, scale=-0.5).then_inc(done, 1)

            act.wait_ge(S["weights_in"], 16 * NW)
            act.wait_ge(S["tables_in"], 16)
            act.activation(negA[:, :, :], negA[:, :, :], ACT.Exp).then_inc(S["expA"], 1)
            act.wait_ge(S["expA"], 1)
            act.activation(negA[:, :, :], negA[:, :, :], ACT.Copy, scale=-1.0).then_inc(S["negA_ready"], 1)
            act.activation(pick_s[:, :, :], pick_f[:, :].rearrange("p (n m) -> p n m", m=P), ACT.Copy
                           ).then_inc(S["pick_cast"], 1)
            act.wait_ge(S["fT_ps"], 1)
            copy(fT[:, :, :], PM[:, 0, 0:2 * P].rearrange("p (a m) -> p a m", m=P)).then_inc(S["fT_sb"], 1)
            act.wait_ge(S["ffnM_ps"], 1)
            copy(ffnM[:, :], PM[:, 1, 0:P]).then_inc(S["ffnM_sb"], 1)
            act.wait_ge(S["negA_ready"], 1)
            act.wait_ge(S["nconvb_ready"], 1)
            act.wait_ge(S["zeros_ready"], 1)

            def front(b):
                act_a.start(b)
                first_rstd(b, act_a, a_mv, a_rs, S["a_var"], S["a_rs0"])
                act.wait_ge(S["a_xT_ps"], b + 1)
                copy(a_xT[:, :], PA[:, 0, 0:T]).then_inc(S["a_xT_ready"], 1)
                act.wait_ge(S["qk_ps"], b + 1)
                copy(qkT[:, :, :], PA[:, 1, :].rearrange("p (a t) -> p a t", a=2)).then_inc(S["qk_ready"], 1)
                act.wait_ge(S["L_sub"], b + 1)
                act.activation(EL[:, :, :, :], EL[:, :, :, :], ACT.Exp).then_inc(S["L_exp"], 1)

            def lifted_L(b):
                act.wait_ge(S["LT_ps"], b * TT + 1)
                copy(ELT[:, 0, :, :], PA[:, 0:2, :].rearrange("p a (q m) -> p (a q) m", m=P)
                     ).then_inc(S["LT_act"], 1)
                act.wait_ge(S["K_sub"], b + 1)
                act.activation(Ks[:, :, :], Ks[:, :, :], ACT.Exp).then_inc(S["K_exp"], 1)
                act.wait_ge(S["N_max"], b + 1)
                for p in range(NP):
                    ins = act.activation(EN[:, p, :], PA[:, p // 2, p % 2 * T:(p % 2 + 1) * T], ACT.Exp,
                                         bias=nmaxN[:, p:p + 1])
                ins.then_inc(S["N_exp"], 1)

            def inverse_start(b):
                act.wait_ge(S["NT_ps"], b * TT + 1)
                copy(ENT[:, 0, :, :], PA[:, 0:2, :].rearrange("p a (q m) -> p (a q) m", m=P)
                     ).then_inc(S["NT_act"], 1)

            def inverse_step(b, j):
                for e in range(2):
                    act.wait_ge(S["M_ready"], b * 2 * NITER + 2 * j + e + 1)
                    for s in range(2):
                        h = slice(s * NL, (s + 1) * NL)
                        ins = copy(Abd[h, 4 * e:4 * e + 4, s * NL:(s + 1) * NL],
                                   PA[h, e, :].rearrange("p (q m) -> p q m", m=P)[:, :, 0:NL], 0.25)
                    ins.then_inc(S["A_bd"], 1)

            def attend(b):
                act.wait_ge(S["yT_ps"], b + 1)
                copy(yT[:, :], PA[:, 1, 0:T]).then_inc(S["yT_ready"], 1)
                first_rstd(b, act_a, a_mv, a_rs, S["f1_var"], S["f1_rs0"])
                act.wait_ge(S["f1_xT_ps"], b + 1)
                copy(a_xT[:, :], PA[:, 0, 0:T]).then_inc(S["f1_xT_ready"], 1)

            def mamba_front(b):
                act_m.start(b)
                first_rstd(b, act_m, m_mv, m_rs, S["m_var"], S["m_rs0"])
                act.wait_ge(S["m_xT_ps"], b + 1)
                copy(xpT[:, KC - 1:KC - 1 + T], PM[:, 0, 0:T]).then_inc(S["m_xT_ready"], 1)
                act.wait_ge(S["in_ps"], b + 1)
                for d in range(DT):
                    act.activation(gate[:, 0, d, :], PM[:, 1, d * T:(d + 1) * T], ACT.Exp,
                                   scale=-1.0, bias=nconvb[:, d:d + 1])
                act.activation(gate[:, 1, :, :], PM[:, 2, :].rearrange("p (d t) -> p d t", t=T), ACT.Exp,
                               scale=-1.0).then_inc(S["gate_exp"], 1)
                act.wait_ge(S["gate_cut"], b + 1)
                link = act_m
                link(act, act.activation(gate[:, :, :, :], gate[:, :, :, :], ACT.Ln, bias=const("one")))
                act.activation(gate[:, :, :, :], gate[:, :, :, :], ACT.Exp, scale=-1.0
                               ).then_inc(S["gate_ready"], 1)
                act.wait_ge(S["dbl_ps"], b + 1)
                copy(dlr[:, :], PM[0:RK, 0, 0:T]).then_inc(S["dlr_ready"], 1)
                copy(bc[:, :, :], PM[0:3 * NS, 3, :].rearrange("p (s t) -> p s t", t=T))
                copy(bch[:, :, :], PM[0:3 * NS, 3, :].rearrange("p (s t) -> p s t", t=T)
                     ).then_inc(S["bc_hi"], 1)
                act.wait_ge(S["dt_ps"], b + 1)
                for d in range(DT):
                    ins = act.activation(spa[:, d, :], PM[:, 1, d * T:(d + 1) * T], ACT.Abs,
                                         bias=bdt[:, d:d + 1])
                ins.then_inc(S["abs_read"], 1)
                act.wait_ge(S["abs_read"], b + 1)
                link(act, act.activation(spa[:, :, :], spa[:, :, :], ACT.Exp, scale=-1.0))
                act.activation(spa[:, :, :], spa[:, :, :], ACT.Ln, bias=const("one")).then_inc(S["sp_ready"], 1)
                act.wait_ge(S["delta_ready"], b + 1)

            def mamba_unit(b, k):
                d, q = k % DT, k // DT
                if k >= 2:
                    act.wait_ge(S["h_ready"], b * NU + k - 1)
                for n in range(NQ):
                    ins = act.activation(dA[:, k % 2, n, 1:T], delta[:, d, 1:T], ACT.Exp,
                                         scale=negA[:, d, NQ * q + n:NQ * q + n + 1])
                ins.then_inc(S["dA_ready"], 1)
                if d == 0:
                    for h in range(NQ // 2):
                        act.wait_ge(S["c_ps"], b * NS // 2 + 2 * q + h + 1)
                        copy(c_sb[:, NQ * q + 2 * h:NQ * q + 2 * h + 2, :],
                             PM[:, 2, :].rearrange("p (n t) -> p n t", t=T)).then_inc(S["c_ready"], 1)

            def mamba_out(b):
                first_rstd(b, act_m, m_mv, m_rs, S["f2_var"], S["f2_rs0"])
                act.wait_ge(S["f2_xT_ps"], b + 1)
                copy(f_xT[:, :], PM[:, 1, 0:T]).then_inc(S["f2_xT_ready"], 1)

            def attention(b, unit):
                front(b)
                unit(0)
                lifted_L(b)
                unit(1)
                inverse_start(b)
                for j in range(NITER):
                    inverse_step(b, j)
                    unit(2 + j)

            attention(0, lambda k: None)
            attend(0)
            with act.Fori(1, B) as i:
                mamba_front(i - 1)
                attention(i, lambda k: mamba_unit(i - 1, k))
                mamba_out(i - 1)
                attend(i)
            mamba_front(B - 1)
            for k in range(NU):
                mamba_unit(B - 1, k)
            mamba_out(B - 1)

        @block.gpsimd
        def _(pool):
            pool.memset(Abd[:, :, :], 0.0)
            pool.memset(zp[:, :, :], 0.0)
            pool.memset(dA[:, :, :, :], 0.0)
            pool.memset(xpT[:, :], 0.0)
            pool.memset(v1[:, :, :, :], 1.0).then_inc(S["filled"], 1)
            pool.wait_ge(S["filled"], 1)
            pool.memset(zp[0:NL, :, HS], 1.0)
            pool.memset(zp[NL:P, :, VC + HS], 1.0).then_inc(S["zeros_ready"], 1)

            def block_diagonal(dst, src):
                n = src.shape[1]
                mask = const("halfones").rearrange("p (s m) -> p s m", m=NL)
                return pool.tensor_tensor(dst.rearrange("p q (s m) -> p q s m", m=NL),
                                          src[:, :, 0:NL].unsqueeze(2).broadcast_to([P, n, 2, NL]),
                                          mask.unsqueeze(1).broadcast_to([P, n, 2, NL]), ALU.mult)

            def inverse_start(b):
                pool.wait_ge(S["K_ready"], b + 1)
                block_diagonal(Kbd[:, :, :], Ks[:, :, :]).then_inc(S["Kbd_ready"], 1)
                pool.wait_ge(S["Y_ready"], b + 1)
                for e in range(2):
                    block_diagonal(Ybd[:, 4 * e:4 * e + 4, :], Yz[:, 4 * e:4 * e + 4, :]
                                   ).then_inc(S["Ybd_ready"], 1)

            def inverse_step(b, j):
                if j < NITER - 1:
                    for e in range(2):
                        pool.wait_ge(S["YZ_ready"], b * 2 * (NITER - 1) + 2 * j + e + 1)
                        block_diagonal(Ybd[:, 4 * e:4 * e + 4, :], Yz[:, 4 * e:4 * e + 4, :]
                                       ).then_inc(S["Ybd_ready"], 1)

            def biased(b, dst, src, ready, done):
                pool.wait_ge(ready, b + 1)
                pool.tensor_tensor(dst[:, :, :], src[:, :, :], bias_b[:, :].unsqueeze(1).broadcast_to([P, TT, C]),
                                   ALU.add).then_inc(done, 1)

            def mamba_front(b):
                pool.wait_ge(S["delta_ready"], b + 1)
                pool.tensor_tensor(du[:, :, :], delta[:, :, :], u[:, :, :], ALU.mult).then_inc(S["du_ready"], 1)

            def mamba_unit(b, k):
                d, q = k % DT, k // DT
                pool.wait_ge(S["h_ready"], b * NU + k + 1)
                pool.wait_ge(S["c_ready"], b * NS // 2 + 2 * q + 2)
                if k >= 2:
                    pool.wait_ge(S["y_acc"], b * NU + k - 1)
                pool.tensor_tensor(hc[:, k % 2, :, :], hst[:, k % 2, :, :], c_sb[:, NQ * q:NQ * (q + 1), :],
                                   ALU.mult).then_inc(S["hc_ready"], 1)

            def attention(b, unit):
                unit(0)
                unit(1)
                inverse_start(b)
                for j in range(NITER):
                    inverse_step(b, j)
                    unit(2 + j)

            pool.wait_ge(S["weights_in"], 16 * NW)
            pool.wait_ge(S["tables_in"], 16)
            attention(0, lambda k: None)
            biased(0, x1b, x1, S["x1_ready"], S["x1b_ready"])
            with pool.Fori(1, B) as i:
                mamba_front(i - 1)
                attention(i, lambda k: mamba_unit(i - 1, k))
                biased(i - 1, x3b, x3, S["x3_ready"], S["x3b_ready"])
                biased(i, x1b, x1, S["x1_ready"], S["x1b_ready"])
            mamba_front(B - 1)
            for k in range(NU):
                mamba_unit(B - 1, k)
            biased(B - 1, x3b, x3, S["x3_ready"], S["x3b_ready"])

        @block.vector
        def _(dve):
            dve.wait_ge(S["weights_in"], 16 * NW)
            dve.wait_ge(S["tables_in"], 16)
            dve.tensor_tensor(wconv[:, :, :], convw_b[:, :, :],
                              win[:, 0:DI].unsqueeze(1).broadcast_to([P, KC, DI]), ALU.mult
                              ).then_inc(S["convw_ready"], 1)
            for s in range(2):
                for r in range(3):
                    ins = dve.tensor_copy(wx3[:, :, s, r, :], wx[:, :, RK + s * NS:RK + (s + 1) * NS])
            ins.then_inc(S["wx3_ready"], 1)
            dve.tensor_scalar(nconvb[:, :], convb[:, :], -1.0, None, ALU.mult).then_inc(S["nconvb_ready"], 1)

            def statistics(b, link, src, st, mv, done):
                for t in range(TT):
                    ins = dve.bn_stats(st[:, t, :], src[:, t, :])
                link(dve, ins)
                dve.memset(pause[:, :], 0.0)
                for t in range(TT):
                    ins = dve.bn_aggr(mv[:, t, :], st[:, t, :])
                ins.then_inc(done, 1)

            def normalise(b, link, src, mv, rs, rs0, dst, done):
                dve.wait_ge(rs0, b + 1)
                link(dve, dve.tensor_tensor(rs[:, 2, :], rs[:, 1, :], rs[:, 1, :], ALU.mult))
                link(dve, dve.scalar_tensor_tensor(out=rs[:, 3, :], in0=mv[:, :, 1], scalar=EPS,
                                                   in1=rs[:, 2, :], op0=ALU.add, op1=ALU.mult))
                link(dve, dve.tensor_scalar(rs[:, 2, :], rs[:, 3, :], -0.5, 1.5, ALU.mult, ALU.add))
                link(dve, dve.tensor_tensor(rs[:, 3, :], rs[:, 2, :], rs[:, 1, :], ALU.mult))
                for t in range(TT):
                    ins = dve.tensor_scalar(dst[:, t, :], src[:, t, :], mv[:, t, 0:1], rs[:, 3, t:t + 1],
                                            ALU.subtract, ALU.mult)
                ins.then_inc(done, 1)

            def spread(ap, n):
                return ap.unsqueeze(2).broadcast_to([ap.shape[0], ap.shape[1], n])

            def front(b):
                dve_a.start(b)
                dve.wait_ge(S["x_in"], 16 * b + 16)
                statistics(b, dve_a, xin, a_st, a_mv, S["a_var"])
                normalise(b, dve_a, xin, a_mv, a_rs, S["a_rs0"], a_xn, S["a_xn_ready"])
                dve.wait_ge(S["v_ps"], b + 1)
                dve.tensor_copy(v1[:, :, :, 0:HS].rearrange("p t h d -> p (t h) d"),
                                PA[:, 2, 0:T].rearrange("p (t d) -> p t d", d=HS)
                                ).then_inc(S["v_ready"], 1)
                dve.wait_ge(S["qk_ready"], b + 1)
                dve_a(dve, dve.tensor_reduce(lm[:, :, :].rearrange("p a l -> p (a l)"),
                                             qkT[:, :, :].rearrange("p a (l r) -> p (a l) r", r=POOLED),
                                             AX.X, ALU.add))
                dve.tensor_tensor(qz[:, :, :], lm[:, 0, :].unsqueeze(1).broadcast_to([P, 4, NL]),
                                  spread(const("headmask"), NL), ALU.mult)
                dve.tensor_scalar(klu[:, :], lm[:, 1, :], 1.0 / POOLED, None, ALU.mult)
                dve.tensor_tensor(kz[:, :, :], lm[:, 1, :].unsqueeze(1).broadcast_to([P, 4, NL]),
                                  spread(const("headmask"), NL), ALU.mult).then_inc(S["lm_ready"], 1)
                dve.wait_ge(S["L_ps"], b + 1)
                flat = PA[:, :, :].rearrange("p a (j m) -> p (a j) m", m=NL)
                dve_a(dve, dve.tensor_reduce(nmaxL[:, :], flat, AX.X, ALU.max, negate=True))
                dve.tensor_tensor(EL[:, :, :, :].rearrange("p g t (j m) -> p (g t j) m", m=NL), flat,
                                  spread(nmaxL[:, :], NL), ALU.add).then_inc(S["L_sub"], 1)

            def softmax_K(b):
                dve.wait_ge(S["LT_ps"], b * TT + 2)
                dve.tensor_copy(ELT[:, 1, :, :], PA[:, 2:4, :].rearrange("p a (q m) -> p (a q) m", m=P)
                                ).then_inc(S["LT_dve"], 1)
                dve.wait_ge(S["K_ps"], b + 1)
                sc = PA[:, :, 0:2 * NL].rearrange("p g (j m) -> p g j m", m=NL)
                dve_a(dve, dve.tensor_reduce(nmaxK[:, :].rearrange("p (g j) -> p g j", j=2), sc,
                                             AX.X, ALU.max, negate=True))
                dve.tensor_tensor(Ks[:, :, :].rearrange("p (g j) m -> p g j m", j=2), sc,
                                  nmaxK[:, :].rearrange("p (g j) -> p g j", j=2).unsqueeze(3)
                                  .broadcast_to([P, 4, 2, NL]), ALU.add).then_inc(S["K_sub"], 1)
                dve.wait_ge(S["N_ps"], b + 1)
                dve.tensor_reduce(nmaxN[:, :], PA[:, :, :].rearrange("p g (j t) -> p (g j) t", t=T),
                                  AX.X, ALU.max, negate=True).then_inc(S["N_max"], 1)
                dve.wait_ge(S["K_exp"], b + 1)
                dve_a(dve, dve.tensor_reduce(sumK[:, :], Ks[:, :, :], AX.X, ALU.add))
                dve_a(dve, dve.reciprocal(rsumK[:, :], sumK[:, :]))
                dve.tensor_tensor(Ks[:, :, :], Ks[:, :, :], spread(rsumK[:, :], NL), ALU.mult
                                  ).then_inc(S["K_ready"], 1)

            def inverse_start(b):
                dve.wait_ge(S["NT_ps"], b * TT + 2)
                dve.tensor_copy(ENT[:, 1, :, :], PA[:, 2:4, :].rearrange("p a (q m) -> p (a q) m", m=P)
                                ).then_inc(S["NT_dve"], 1)
                dve.wait_ge(S["cy_ps"], b + 1)
                dve_a(dve, dve.tensor_reduce(den[:, :], PA[:, 0, :].rearrange("p (q m) -> p q m", m=NL),
                                             AX.X, ALU.max))
                dve_a(dve, dve.reciprocal(rden[:, :], den[:, :]))
                dve.tensor_tensor(Yz[:, :, 0:NL], PA[:, 1, :].rearrange("p (q m) -> p q m", m=NL),
                                  spread(rden[:, :], NL), ALU.mult).then_inc(S["Y_ready"], 1)
                dve.wait_ge(S["nv_ps"], b + 1)
                nv = PA[:, 2, 0:NP * 2 * VC].rearrange("p (q c) -> p q c", c=2 * VC)
                for s in range(2):
                    ins = dve.reciprocal(rsumN[s * NL:(s + 1) * NL, :], nv[s * NL:(s + 1) * NL, :, s * VC + HS])
                dve_a(dve, ins)
                for s in range(2):
                    ins = dve.tensor_tensor(wv[s * NL:(s + 1) * NL, :, :],
                                            nv[s * NL:(s + 1) * NL, :, s * VC:s * VC + HS],
                                            spread(rsumN[s * NL:(s + 1) * NL, :], HS), ALU.mult)
                ins.then_inc(S["w_ready"], 1)
                dve.wait_ge(S["z0_ps"], b + 1)
                dve.tensor_tensor(Yz[:, :, NL:ZC], PA[:, 3, 0:NP * HS].rearrange("p (q c) -> p q c", c=HS),
                                  spread(rden[:, :], HS), ALU.mult).then_inc(S["z_ready"], 1)
                dve.wait_ge(S["z_ready"], b + 1)

            def inverse_step(b, j):
                last = j == NITER - 1
                c0 = NL if last else 0
                for e in range(2):
                    dve.wait_ge(S["sq_ps"], b * 2 * NITER + 2 * j + e + 1)
                    q = slice(4 * e, 4 * e + 4)
                    au = PA[:, e, :].rearrange("p (q m) -> p q m", m=P)[:, :, c0:ZC]
                    dve.scalar_tensor_tensor(out=Hz[:, q, c0:ZC], in0=au, scalar=-15.0 / 13.0,
                                             in1=Yz[:, q, c0:ZC], op0=ALU.mult, op1=ALU.add)
                    dve.scalar_tensor_tensor(out=Mr[:, q, c0:ZC], in0=Yz[:, q, c0:ZC], scalar=-7.0,
                                             in1=au, op0=ALU.mult, op1=ALU.add
                                             ).then_inc(S["M_ready"], 1)
                for e in range(2):
                    dve.wait_ge(S["cube_ps"], b * 2 * NITER + 2 * j + e + 1)
                    q = slice(4 * e, 4 * e + 4)
                    cu = PA[:, 2 + e, :].rearrange("p (q m) -> p q m", m=P)
                    if last:
                        for s in range(2):
                            h = slice(s * NL, (s + 1) * NL)
                            ins = dve.scalar_tensor_tensor(out=zp[h, q, s * VC:s * VC + HS],
                                                           in0=Hz[h, q, NL:ZC], scalar=3.25,
                                                           in1=cu[h, :, NL:ZC], op0=ALU.mult, op1=ALU.subtract)
                        if e == 1:
                            ins.then_inc(S["zp_ready"], 1)
                    else:
                        dve.scalar_tensor_tensor(out=Yz[:, q, :], in0=Hz[:, q, :], scalar=3.25,
                                                 in1=cu[:, :, 0:ZC], op0=ALU.mult, op1=ALU.subtract
                                                 ).then_inc(S["YZ_ready"], 1)

            def attend(b):
                dve.wait_ge(S["y_ps"], b + 1)
                yp = PA[:, 0, 0:TT * NH * VC].rearrange("p (t c) -> p t c", c=VC)
                dve_a(dve, dve.reciprocal(rsumL[:, :], yp[:, :, HS]))
                dve.tensor_tensor(yat[:, :, :, :].rearrange("p t h d -> p (t h) d"), yp[:, :, 0:HS],
                                  spread(rsumL[:, :], HS), ALU.mult).then_inc(S["y_ready"], 1)
                dve.wait_ge(S["proj_ps"], b + 1)
                dve.tensor_tensor(x1[:, :, :], xin[:, :, :], PA[:, 2, 0:T].rearrange("p (t c) -> p t c", c=C),
                                  ALU.add).then_inc(S["x1_ready"], 1)
                dve.wait_ge(S["x1_ready"], b + 1)
                statistics(b, dve_a, x1, a_st, a_mv, S["f1_var"])
                normalise(b, dve_a, x1, a_mv, a_rs, S["f1_rs0"], a_xn, S["f1_xn_ready"])
                dve.wait_ge(S["f1_ps"], b + 1)
                dve.wait_ge(S["x1b_ready"], b + 1)
                dve.tensor_tensor(x2[:, :, :], x1b[:, :, :], PA[:, 1, 0:T].rearrange("p (t c) -> p t c", c=C),
                                  ALU.add).then_inc(S["x2_ready"], 1)

            def mamba_front(b):
                dve_m.start(b)
                dve.wait_ge(S["x2_ready"], b + 1)
                statistics(b, dve_m, x2, m_st, m_mv, S["m_var"])
                normalise(b, dve_m, x2, m_mv, m_rs, S["m_rs0"], m_xn, S["m_xn_ready"])
                dve.wait_ge(S["gate_exp"], b + 1)
                dve.tensor_scalar(gate[:, :, :, :], gate[:, :, :, :], LN_MOST, None, ALU.min
                                  ).then_inc(S["gate_cut"], 1)
                dve.wait_ge(S["gate_ready"], b + 1)
                for d in range(DT):
                    ins = dve.scalar_tensor_tensor(out=u[:, d, :], in0=PM[:, 1, d * T:(d + 1) * T],
                                                   scalar=convb[:, d:d + 1], in1=gate[:, 0, d, :],
                                                   op0=ALU.add, op1=ALU.mult)
                ins.then_inc(S["u_ready"], 1)
                dve.tensor_tensor(sres[:, :, :], PM[:, 2, :].rearrange("p (d t) -> p d t", t=T),
                                  gate[:, 1, :, :], ALU.mult)
                dve.wait_ge(S["bc_hi"], b + 1)
                dve_m(dve, dve.scalar_tensor_tensor(out=bc[:, :, :], in0=bch[:, :, :],
                                                    scalar=const("part1")[0:3 * NS, :], in1=bc[:, :, :],
                                                    op0=ALU.mult, op1=ALU.add))
                dve_m(dve, dve.tensor_copy(bch[:, :, :], bc[:, :, :]))
                dve.scalar_tensor_tensor(out=bcs[:, :, :], in0=bch[:, :, :],
                                         scalar=const("part2")[0:3 * NS, :], in1=bc[:, :, :],
                                         op0=ALU.mult, op1=ALU.add).then_inc(S["bc_ready"], 1)
                dve.wait_ge(S["abs_read"], b + 1)
                for d in range(DT):
                    ins = dve.tensor_scalar(spp[:, d, :], PM[:, 1, d * T:(d + 1) * T], bdt[:, d:d + 1], 0.0,
                                            ALU.add, ALU.max)
                dve_m(dve, ins)
                dve.wait_ge(S["sp_ready"], b + 1)
                dve.tensor_tensor(delta[:, :, :], spp[:, :, :], spa[:, :, :], ALU.add
                                  ).then_inc(S["delta_ready"], 1)
                dve.wait_ge(S["du_ready"], b + 1)

            def mamba_unit(b, k):
                d, q = k % DT, k // DT
                if d == 0:
                    dve.wait_ge(S["b_ps"], b * NS // NQ + q + 1)
                if k >= 2:
                    dve.wait_ge(S["h_ready"], b * NU + k - 1)
                dve.tensor_tensor(dBu[:, k % 2, :, :], PM[:, 0:2, :].rearrange("p a (n t) -> p (a n) t", t=T),
                                  du[:, d, :].unsqueeze(1).broadcast_to([P, NQ, T]), ALU.mult
                                  ).then_inc(S["dBu_ready"], 1)
                dve.wait_ge(S["dBu_ready"], b * NU + k + 1)
                dve.wait_ge(S["dA_ready"], b * NU + k + 1)
                if k >= 2:
                    dve.wait_ge(S["hc_ready"], b * NU + k - 1)
                dve.tensor_tensor_scan(hst[:, k % 2, :, :].rearrange("p n t -> p (n t)"),
                                       dA[:, k % 2, :, :].rearrange("p n t -> p (n t)"),
                                       dBu[:, k % 2, :, :].rearrange("p n t -> p (n t)"),
                                       0.0, ALU.mult, ALU.add).then_inc(S["h_ready"], 1)

            def mamba_out(b):
                dve.wait_ge(S["y_acc"], b * NU + NU)
                for d in range(DT):
                    ins = dve.scalar_tensor_tensor(out=ym[:, d, :], in0=u[:, d, :], scalar=dskip[:, d:d + 1],
                                                   in1=PM[:, 3, d * T:(d + 1) * T], op0=ALU.mult, op1=ALU.add)
                dve_m(dve, ins)
                dve.tensor_tensor(ym[:, :, :], ym[:, :, :], sres[:, :, :], ALU.mult).then_inc(S["ym_ready"], 1)
                dve.wait_ge(S["out_ps"], b + 1)
                dve.tensor_tensor(x3[:, :, :], x2[:, :, :], PM[:, 0, 0:T].rearrange("p (t c) -> p t c", c=C),
                                  ALU.add).then_inc(S["x3_ready"], 1)
                dve.wait_ge(S["x3_ready"], b + 1)
                statistics(b, dve_m, x3, m_st, m_mv, S["f2_var"])
                normalise(b, dve_m, x3, m_mv, m_rs, S["f2_rs0"], m_xn, S["f2_xn_ready"])
                dve.wait_ge(S["f2_ps"], b + 1)
                dve.wait_ge(S["x3b_ready"], b + 1)
                if isinstance(b, int):
                    dve.wait_ge(S["x_out"], 16 * b)
                dve.tensor_tensor(x4[:, :, :], x3b[:, :, :], PM[:, 2, 0:T].rearrange("p (t c) -> p t c", c=C),
                                  ALU.add).then_inc(S["x4_ready"], 1)

            def attention(b, unit):
                front(b)
                unit(0)
                softmax_K(b)
                unit(1)
                inverse_start(b)
                for j in range(NITER):
                    inverse_step(b, j)
                    unit(2 + j)

            dve.wait_ge(S["zeros_ready"], 1)
            attention(0, lambda k: None)
            attend(0)
            with dve.Fori(1, B) as i:
                mamba_front(i - 1)
                attention(i, lambda k: mamba_unit(i - 1, k))
                mamba_out(i - 1)
                attend(i)
            mamba_front(B - 1)
            for k in range(NU):
                mamba_unit(B - 1, k)
            mamba_out(B - 1)


_INS = ['L0_attn_a_x', 'L0_attn_a_W_attn', 'L0_attn_a_W_proj', 'L0_attn_b_W_in', 'L0_attn_b_conv_w',
        'L0_attn_b_conv_b', 'L0_attn_b_W_x', 'L0_attn_b_W_dt', 'L0_attn_b_b_dt', 'L0_attn_b_A_log',
        'L0_attn_b_D', 'L0_attn_b_W_out', 'L0_ffn_w_freq_real', 'L0_ffn_w_freq_imag', 'L0_ffn_bias']


def kernel(**inputs):
    import numpy as _np
    import concourse.bacc as _bacc
    from concourse import mybir as _mybir
    from concourse.bass_utils import run_bass_kernel_spmd as _run

    nc = _bacc.Bacc("TRN2", target_bir_lowering=False, num_devices=1)
    tab, pick = shape_tables()
    arrays, args = {}, []
    for name, a in [(n, inputs[n]) for n in _INS] + [("tab", tab), ("pick", pick)]:
        a = _np.ascontiguousarray(a)
        arrays[f"in_{name}"] = a
        args.append(nc.dram_tensor(f"in_{name}", a.shape, _mybir.dt.from_np(a.dtype), kind="ExternalInput").ap())
    args.append(nc.dram_tensor("out_x", (B, T, C), F32, kind="ExternalOutput").ap())
    hybrid_layer_kernel(nc, *args)
    r = _run(nc, [arrays], core_ids=[0])
    return r.results[0]["out_x"]
```

```python
from contextlib import ExitStack

import numpy as np

import concourse.bass as bass
from concourse import mybir

F32 = mybir.dt.float32
BF16 = mybir.dt.bfloat16
ALU = mybir.AluOpType
ACT = mybir.ActivationFunctionType
AX = mybir.AxisListType

P = 128
B, T, C = 16, 256, 128
TT = T // P
NH, HS, NL = 16, 8, 64
NP = NH // 2
POOLED = T // NL
NITER = 6
ZC = NL + HS
VC = HS + 1
DI, DT = 256, 2
NS, RK, KC = 16, 64, 4
NQ = 2
NU = NS // NQ
SLOTS = 17
UNIT_AT = {0: 0, 1: 1, 3: 2, 4: 3, 6: 4, 7: 5, 9: 6, 10: 7}
DVE_LINKS = (15, 6, 8, 6)
ACT_LINKS = (1, 1, 3, 1)
EPS = 1e-5
LN_MOST = 2.0 ** 62

TAB = {}
_at = 0
for _name, _n in (("ident", P), ("halfones", P), ("cos", P), ("sin", P), ("nsin", P), ("icos", P),
                  ("insin", P), ("headmask", 4), ("part1", 1), ("part2", 1), ("eps", 1), ("one", 1)):
    TAB[_name] = (_at, _at + _n)
    _at += _n
TABW = _at


def shape_tables():
    tab = np.zeros((P, TABW), np.float32)
    p = np.arange(P)
    angle = 2 * np.pi * (np.outer(p, p) % C) / C

    def put(name, a):
        tab[:, TAB[name][0]:TAB[name][1]] = a
    put("ident", np.eye(P))
    put("halfones", (p[:, None] // NL == p[None, :] // NL))
    put("cos", np.cos(angle))
    put("sin", np.sin(angle))
    put("nsin", -np.sin(angle))
    put("icos", np.cos(angle) / C)
    put("insin", -np.sin(angle) / C)
    put("headmask", (p[:, None] // HS % 4 == np.arange(4)[None, :]) / POOLED)
    put("part1", -(p[:, None] // NS >= 1).astype(np.float32))
    put("part2", -(p[:, None] // NS >= 2).astype(np.float32))
    put("eps", EPS)
    put("one", 1.0)
    pick = np.zeros((3 * NS, NS, P), np.float32)
    for r in range(3 * NS):
        pick[r, r % NS, :] = 1.0
    return tab, pick.reshape(3 * NS, NS * P)


class Link:

    def __init__(self, sem, per_batch):
        self.sem, self.per_batch = sem, per_batch

    def start(self, b):
        self.base, self.n = b * self.per_batch, 0

    def __call__(self, eng, ins):
        self.n += 1
        ins.then_inc(self.sem, 1)
        eng.wait_ge(self.sem, self.base + self.n)


def hybrid_layer_kernel(nc, x, W_attn, W_proj, W_in, conv_w, conv_b, W_x, W_dt, b_dt, A_log, D, W_out,
                        w_re, w_im, bias, tab, pick, out):
    ctx = ExitStack()
    with ctx:
        def sb(name, shape, dt=F32):
            return ctx.enter_context(nc.sbuf_tensor(name, shape, dt))

        def sem(name):
            return ctx.enter_context(nc.semaphore(name))

        tb = sb("tb", [P, TABW])
        pick_f = sb("pick_f", [3 * NS, NS * P])
        pick_s = sb("pick_s", [3 * NS, NS, P], BF16)
        wqkv = sb("wqkv", [P, 3 * C])
        wproj = sb("wproj", [P, C])
        win = sb("win", [P, 2 * DI])
        convw_b = sb("convw_b", [P, KC, DI])
        wconv = sb("wconv", [P, KC, DI])
        convb = sb("convb", [P, DT])
        wx = sb("wx", [P, DT, RK + 2 * NS])
        wx3 = sb("wx3", [P, DT, 2, 3, NS])
        wdt = sb("wdt", [RK, DI])
        bdt = sb("bdt", [P, DT])
        negA = sb("negA", [P, DT, NS])
        dskip = sb("dskip", [P, DT])
        wout = sb("wout", [P, DT, C])
        wre = sb("wre", [P, P])
        wim = sb("wim", [P, P])
        fT = sb("fT", [P, 2, P])
        ffnM = sb("ffnM", [P, P])
        bias_b = sb("bias_b", [P, C])

        def const(name):
            return tb[:, TAB[name][0]:TAB[name][1]]
        ident = const("ident")

        xin = sb("xin", [P, TT, C])
        a_xn = sb("a_xn", [P, TT, C])
        a_xT = sb("a_xT", [P, T])
        qkT = sb("qkT", [P, 2, T])
        v1 = sb("v1", [P, TT, NH, VC])
        lm = sb("lm", [P, 2, NL])
        qz = sb("qz", [P, 4, NL])
        kz = sb("kz", [P, 4, NL])
        klu = sb("klu", [P, NL])
        nmaxL = sb("nmaxL", [P, 2 * TT * 4])
        EL = sb("EL", [P, 2, TT, 4 * NL])
        nmaxN = sb("nmaxN", [P, NP])
        EN = sb("EN", [P, 4, T])
        ENT = sb("ENT", [P, TT, NP, P])
        nmaxK = sb("nmaxK", [P, NP])
        Ks = sb("Ks", [P, NP, NL])
        sumK = sb("sumK", [P, NP])
        rsumK = sb("rsumK", [P, NP])
        den = sb("den", [P, NP])
        rden = sb("rden", [P, NP])
        Kbd = sb("Kbd", [P, NP, P])
        rsumN = sb("rsumN", [P, NP])
        wv = sb("wv", [P, NP, HS])
        ELT = sb("ELT", [P, TT, NP, P])
        Yz = sb("Yz", [P, NP, ZC])
        Ybd = sb("Ybd", [P, NP, P])

        xres = sb("xres", [P, TT, C])
        Hz = sb("Hz", [P, NP, ZC])
        Mr = sb("Mr", [P, NP, ZC])
        Abd = sb("Abd", [P, NP, P])
        zp = sb("zp", [P, NP, 2 * VC])
        rsumL = sb("rsumL", [P, TT * NH])
        yat = sb("yat", [P, TT, NH, HS])
        yT = sb("yT", [P, T])
        x1 = sb("x1", [P, TT, C])
        x1b = sb("x1b", [P, TT, C])
        f_xn = sb("f_xn", [P, TT, C])
        f_xT = sb("f_xT", [P, T])
        x2 = sb("x2", [P, TT, C])

        m_xn = sb("m_xn", [P, TT, C])
        xpT = sb("xpT", [P, KC - 1 + T])
        vr = sb("vr", [P, 2, DT, T])
        gate = sb("gate", [P, 2, DT, T])
        u = sb("u", [P, DT, T])
        dlr = sb("dlr", [RK, T])
        bc = sb("bc", [3 * NS, 2, T])
        bch = sb("bch", [3 * NS, 2, T], BF16)
        spa = sb("spa", [P, DT, T])
        spp = sb("spp", [P, DT, T])
        delta = sb("delta", [P, DT, T])
        du = sb("du", [P, DT, T])
        bcs = sb("bcs", [3 * NS, 2, T], BF16)
        uD = sb("uD", [P, DT, T])
        sres = sb("sres", [P, DT, T])
        x2b = sb("x2b", [P, TT, C])

        c_sb = sb("c_sb", [P, 2, NQ, T])
        dA = sb("dA", [P, 2, DT, NQ, T])
        dBu = sb("dBu", [P, 2, DT, NQ, T])
        hst = sb("hst", [P, 2, DT, NQ, T])
        hc = sb("hc", [P, DT, NQ, T])
        hs = sb("hs", [P, 2, DT, T])
        ysum = sb("ysum", [P, DT, T])
        ym = sb("ym", [P, DT, T])
        x3 = sb("x3", [P, TT, C])
        x3b = sb("x3b", [P, TT, C])
        g_xn = sb("g_xn", [P, TT, C])
        g_xT = sb("g_xT", [P, T])
        x4 = sb("x4", [P, TT, C])

        pause = sb("pause", [P, 1])
        st = [sb(f"st{n}", [P, TT, 6]) for n in range(4)]
        mv = [sb(f"mv{n}", [P, TT, 2]) for n in range(4)]
        rs = [sb(f"rs{n}", [P, 4, TT]) for n in range(4)]

        PS = ctx.enter_context(nc.psum_tensor("PS", [P, 8, 512], F32))

        names = """weights_in tables_in x_in xres_in x_out
            pick_cast expA negA_ready convw_ready wx3_ready filled zeros_ready fT_ps fT_sb ffnM_ps ffnM_sb
            a_xn_ready a_xT_ps a_xT_ready v_ps v_ready qk_ps qk_ready lm_ready
            K_ps K_sub K_exp K_ready Kbd_ready N_ps N_max N_exp NT_ps NT_act NT_dve nv_ps w_ready
            cy_ps Y_ready z0_ps z_ready L_ps L_sub L_exp LT_ps LT_act LT_dve
            Ybd_ready sq_ps A_bd M_ready cube_ps YZ_ready zp_ready
            y_ps y_ready yT_ps yT_ready proj_ps x1_ready x1b_ready f_xn_ready f_xT_ps f_xT_ready f_ps x2_ready
            m_xn_ready m_xT_ps m_xT_ready conv_ps conv_out res_ps res_out gate_exp gate_cut gate_ready u_ready
            dlr_ps dlr_ready bc_ps bc_hi bc_ready dt_ps abs_read sp_ready delta_ready du_ready sres_ready x2b_ready
            b_ps c_ps c_ready dA_ready dBu_ready h_ready hc_ready hs_ready y_acc ym_ready out_ps x3_ready x3b_ready
            g_xn_ready g_xT_ps g_xT_ready g_ps x4_ready""".split()
        S = {n: sem(n) for n in names}
        var_ready = [sem(f"var_ready{n}") for n in range(4)]
        rs0_ready = [sem(f"rs0_ready{n}") for n in range(4)]
        dve_link = [Link(sem(f"dve_link{n}"), k) for n, k in enumerate(DVE_LINKS)]
        act_link = [Link(sem(f"act_link{n}"), k) for n, k in enumerate(ACT_LINKS)]
        NW = 15

        block = ctx.enter_context(nc.Block())

        def pipeline(eng, stages):
            order = (3, 1, 0, 2)

            def turn_of_loop(i, lowest, highest):
                for slot in range(SLOTS):
                    for n in order:
                        if lowest <= n <= highest:
                            stages[n](i - n, slot)
            for i in range(3):
                turn_of_loop(i, 0, i)
            with eng.Fori(3, B) as i:
                turn_of_loop(i, 0, 3)
            for i in range(B, B + 3):
                turn_of_loop(i, i - B + 1, 3)

        @block.sync
        def _(sp):
            def tokens(ap, b):
                return ap[bass.ds(b, 1), :, :].rearrange("b (t p) c -> p (b t) c", p=P)

            def load_x(b):
                sp.dma_start(xin[:, :, :], tokens(x, b)).then_inc(S["x_in"], 16)

            def load_residual(b):
                sp.dma_start(xres[:, :, :], tokens(x, b)).then_inc(S["xres_in"], 16)

            def store(b):
                sp.wait_ge(S["x4_ready"], b + 1)
                sp.dma_start(tokens(out, b), x4[:, :, :]).then_inc(S["x_out"], 16)

            sp.dma_start(tb[:, :], tab).then_inc(S["tables_in"], 16)
            load_x(0)
            sp.dma_start(wqkv[:, :], W_attn).then_inc(S["weights_in"], 16)
            sp.dma_start(wproj[:, :], W_proj).then_inc(S["weights_in"], 16)
            sp.dma_start(wre[:, :], w_re).then_inc(S["weights_in"], 16)
            sp.dma_start(wim[:, :], w_im).then_inc(S["weights_in"], 16)
            sp.dma_start(win[:, :], W_in).then_inc(S["weights_in"], 16)
            sp.dma_start(convw_b[:, :, :], conv_w.rearrange("k a d -> a k d").broadcast_to([P, KC, DI])
                         ).then_inc(S["weights_in"], 16)
            sp.dma_start(convb[:, :], conv_b.rearrange("(t p) -> p t", p=P),
                         allow_slow_non_contiguous=True).then_inc(S["weights_in"], 16)
            sp.dma_start(wx[:, :, :], W_x.rearrange("(t p) r -> p t r", p=P)).then_inc(S["weights_in"], 16)
            sp.dma_start(wdt[:, :], W_dt).then_inc(S["weights_in"], 16)
            sp.dma_start(bdt[:, :], b_dt.rearrange("(t p) -> p t", p=P),
                         allow_slow_non_contiguous=True).then_inc(S["weights_in"], 16)
            sp.dma_start(negA[:, :, :], A_log.rearrange("(t p) n -> p t n", p=P)).then_inc(S["weights_in"], 16)
            sp.dma_start(dskip[:, :], D.rearrange("(t p) -> p t", p=P),
                         allow_slow_non_contiguous=True).then_inc(S["weights_in"], 16)
            sp.dma_start(wout[:, :, :], W_out.rearrange("(t p) c -> p t c", p=P)).then_inc(S["weights_in"], 16)
            sp.dma_start(bias_b[:, :], bias.rearrange("(a c) -> a c", a=1).broadcast_to([P, C])
                         ).then_inc(S["weights_in"], 16)
            sp.dma_start(pick_f[:, :], pick).then_inc(S["weights_in"], 16)

            def turn_of_loop(i, with_store):
                if not isinstance(i, int) or i < B + 1:
                    if not isinstance(i, int) or i > 1:
                        sp.wait_ge(S["x1_ready"], i - 1)
                    if not isinstance(i, int) or i > 3:
                        sp.wait_ge(S["x_out"], 16 * (i - 3))
                    if not isinstance(i, int) or i > 0:
                        load_residual(i - 1)
                if not isinstance(i, int) or i < B - 1:
                    sp.wait_ge(S["a_xn_ready"], i + 1)
                    load_x(i + 1)
                if with_store:
                    store(i - 3)

            for i in range(4):
                turn_of_loop(i, i == 3)
            with sp.Fori(4, B - 1) as i:
                turn_of_loop(i, True)
            for i in range(B - 1, B + 3):
                turn_of_loop(i, True)
            sp.wait_ge(S["x_out"], 16 * B)

        @block.tensor
        def _(pe):
            pe.wait_ge(S["tables_in"], 16)
            pe.wait_ge(S["weights_in"], 16 * NW)
            pe.matmul(PS[:, 0, 0:P], wre[:, :], const("cos"), start=True, stop=False)
            pe.matmul(PS[:, 0, 0:P], wim[:, :], const("sin"), start=False, stop=True)
            pe.matmul(PS[:, 0, P:2 * P], wim[:, :], const("cos"), start=True, stop=False)
            pe.matmul(PS[:, 0, P:2 * P], wre[:, :], const("nsin"), start=False, stop=True
                      ).then_inc(S["fT_ps"], 1)
            pe.wait_ge(S["fT_sb"], 1)
            pe.matmul(PS[:, 1, 0:P], fT[:, 0, :], const("icos"), start=True, stop=False)
            pe.matmul(PS[:, 1, 0:P], fT[:, 1, :], const("insin"), start=False, stop=True
                      ).then_inc(S["ffnM_ps"], 1)
            pe.wait_ge(S["ffnM_sb"], 1)
            pe.wait_ge(S["pick_cast"], 1)
            pe.wait_ge(S["convw_ready"], 1)
            pe.wait_ge(S["wx3_ready"], 1)
            pe.wait_ge(S["zeros_ready"], 1)

            def turn(src, bank, done):
                for t in range(TT):
                    mm = pe.transpose(bank[:, t * P:(t + 1) * P], src[:, t, :], ident)
                mm.then_inc(done, 1)

            def project(xT, w, bank, done):
                for t in range(TT):
                    mm = pe.matmul(bank[:, t * C:(t + 1) * C], xT[:, t * P:(t + 1) * P], w,
                                   start=True, stop=True)
                mm.then_inc(done, 1)

            def softmaxes(b, slot):
                if slot == 1:
                    pe.wait_ge(S["a_xn_ready"], b + 1)
                    turn(a_xn, PS[:, 0, :], S["a_xT_ps"])
                if slot == 2:
                    pe.wait_ge(S["a_xT_ready"], b + 1)
                    project(a_xT, wqkv[:, 2 * C:3 * C], PS[:, 1, :], S["v_ps"])
                    for n in range(2):
                        mm = pe.matmul(PS[:, 0, n * T:(n + 1) * T], wqkv[:, n * C:(n + 1) * C], a_xT[:, :],
                                       start=True, stop=True)
                    mm.then_inc(S["qk_ps"], 1)
                if slot in (4, 5):
                    h = slot - 4
                    if h == 0:
                        pe.wait_ge(S["lm_ready"], b + 1)
                    else:
                        pe.wait_ge(S["K_sub"], 2 * b + 1)
                    for jp in range(2):
                        for g in (2 * h, 2 * h + 1):
                            c = slice(32 * g, 32 * g + 32)
                            mm = pe.matmul(PS[:, g % 2, jp * NL:(jp + 1) * NL], qz[c, 2 * jp:2 * jp + 2, :],
                                           klu[c, :], start=True, stop=True)
                    mm.then_inc(S["K_ps"], 1)
                if slot in (6, 8):
                    h = (slot - 6) // 2
                    if h == 0:
                        pe.wait_ge(S["K_sub"], 2 * b + 2)
                    else:
                        pe.wait_ge(S["NT_act"], 2 * b + 1)
                        pe.wait_ge(S["NT_dve"], 2 * b + 1)
                    for jp in range(2):
                        for g in (2 * h, 2 * h + 1):
                            c = slice(32 * g, 32 * g + 32)
                            mm = pe.matmul(PS[:, g % 2, jp * T:(jp + 1) * T], qz[c, 2 * jp:2 * jp + 2, :],
                                           qkT[c, 1, :], start=True, stop=True)
                    mm.then_inc(S["N_ps"], 1)
                if slot in (7, 9):
                    h = (slot - 7) // 2
                    pe.wait_ge(S["N_exp"], 2 * b + h + 1)
                    for t in range(TT):
                        for p in range(4):
                            mm = pe.transpose(PS[:, t, p * P:(p + 1) * P], EN[:, p, t * P:(t + 1) * P], ident)
                        mm.then_inc(S["NT_ps"], 1)
                if slot == 10:
                    pe.wait_ge(S["NT_act"], 2 * b + 2)
                    pe.wait_ge(S["NT_dve"], 2 * b + 2)
                    for p in range(NP):
                        for t in range(TT):
                            mm = pe.matmul(PS[:, 0, p * 2 * VC:(p + 1) * 2 * VC], ENT[:, t, p, :],
                                           v1[:, t, 2 * p:2 * p + 2, :], start=(t == 0), stop=(t == TT - 1))
                    mm.then_inc(S["nv_ps"], 1)
                if slot == 11:
                    pe.wait_ge(S["Kbd_ready"], b + 1)
                    pe.matmul(PS[:, 1, :], const("halfones"), Ks[:, :, :], start=True, stop=True)
                    pe.wait_ge(S["w_ready"], b + 1)
                    for p in range(NP):
                        mm = pe.matmul(PS[:, 0, p * NL:(p + 1) * NL], Kbd[:, p, :], Ks[:, p, :],
                                       start=True, stop=True)
                    mm.then_inc(S["cy_ps"], 1)
                if slot == 12:
                    pe.wait_ge(S["Y_ready"], b + 1)
                    for p in range(NP):
                        mm = pe.matmul(PS[:, 1, p * HS:(p + 1) * HS], Kbd[:, p, :], wv[:, p, :],
                                       start=True, stop=True)
                    mm.then_inc(S["z0_ps"], 1)
                if slot in (13, 15):
                    h = (slot - 13) // 2
                    if h == 0:
                        pe.wait_ge(S["z_ready"], b + 1)
                    else:
                        pe.wait_ge(S["LT_act"], 2 * b + 1)
                        pe.wait_ge(S["LT_dve"], 2 * b + 1)
                    for t in range(TT):
                        for g in (2 * h, 2 * h + 1):
                            c = slice(32 * g, 32 * g + 32)
                            mm = pe.matmul(PS[:, g % 2, t * T:(t + 1) * T], qkT[c, 0, t * P:(t + 1) * P],
                                           kz[c, :, :], start=True, stop=True)
                    mm.then_inc(S["L_ps"], 1)
                if slot in (14, 16):
                    h = (slot - 14) // 2
                    pe.wait_ge(S["L_exp"], 2 * b + h + 1)
                    for t in range(TT):
                        for p in range(4):
                            mm = pe.transpose(PS[:, t, p * P:(p + 1) * P],
                                              EL[:, p // 2, t, p % 2 * P:(p % 2 + 1) * P], ident)
                        mm.then_inc(S["LT_ps"], 1)

            def inverse(b, slot):
                j, cube = slot // 2, slot % 2
                if j < NITER and not cube:
                    if j == 0:
                        pe.wait_ge(S["z_ready"], b + 1)
                        if not isinstance(b, int) or b > 0:
                            pe.wait_ge(S["x2_ready"], b)
                    for e in range(2):
                        pe.wait_ge(S["Ybd_ready"], b * 2 * NITER + 2 * j + e + 1)
                        for p in range(4):
                            q = 4 * e + p
                            mm = pe.matmul(PS[:, 2 + e, p * P:p * P + ZC], Ybd[:, q, :], Yz[:, q, :],
                                           start=True, stop=True)
                        mm.then_inc(S["sq_ps"], 1)
                if j < NITER and cube:
                    c0 = NL if j == NITER - 1 else 0
                    for e in range(2):
                        pe.wait_ge(S["A_bd"], b * 2 * NITER + 2 * j + e + 1)
                        for p in range(4):
                            q = 4 * e + p
                            mm = pe.matmul(PS[:, 2 + e, p * P + c0:p * P + ZC], Abd[:, q, :], Mr[:, q, c0:ZC],
                                           start=True, stop=True)
                        mm.then_inc(S["cube_ps"], 1)
                if slot == 12:
                    pe.wait_ge(S["zp_ready"], b + 1)
                    pe.wait_ge(S["LT_act"], 2 * b + 2)
                    pe.wait_ge(S["LT_dve"], 2 * b + 2)
                    for t in range(TT):
                        for p in range(NP):
                            at = (t * NP + p) * 2 * VC
                            mm = pe.matmul(PS[:, 2, at:at + 2 * VC], ELT[:, t, p, :], zp[:, p, :],
                                           start=True, stop=True)
                    mm.then_inc(S["y_ps"], 1)
                if slot == 13:
                    pe.wait_ge(S["y_ready"], b + 1)
                    turn(yat[:, :, :, :].rearrange("p t h d -> p t (h d)"), PS[:, 3, :], S["yT_ps"])
                if slot == 14:
                    pe.wait_ge(S["yT_ready"], b + 1)
                    project(yT, wproj[:, :], PS[:, 2, :], S["proj_ps"])
                if slot == 15:
                    pe.wait_ge(S["f_xn_ready"], b + 1)
                    turn(f_xn, PS[:, 3, :], S["f_xT_ps"])
                if slot == 16:
                    pe.wait_ge(S["f_xT_ready"], b + 1)
                    project(f_xT, ffnM[:, :], PS[:, 2, :], S["f_ps"])

            def inner(b, slot):
                bank = PS[:, 4, :]
                if slot == 1:
                    pe.wait_ge(S["m_xn_ready"], b + 1)
                    turn(m_xn, bank, S["m_xT_ps"])
                if slot == 2:
                    pe.wait_ge(S["m_xT_ready"], b + 1)
                    for d in range(DT):
                        for k in range(KC):
                            mm = pe.matmul(bank[:, d * T:(d + 1) * T], wconv[:, k, d * P:(d + 1) * P],
                                           xpT[:, k:k + T], start=(k == 0), stop=(k == KC - 1))
                    mm.then_inc(S["conv_ps"], 1)
                if slot == 3:
                    pe.wait_ge(S["conv_out"], b + 1)
                    for d in range(DT):
                        mm = pe.matmul(bank[:, d * T:(d + 1) * T], win[:, DI + d * P:DI + (d + 1) * P],
                                       xpT[:, KC - 1:KC - 1 + T], start=True, stop=True)
                    mm.then_inc(S["res_ps"], 1)
                if slot == 7:
                    pe.wait_ge(S["res_out"], b + 1)
                    pe.wait_ge(S["u_ready"], b + 1)
                    for d in range(DT):
                        mm = pe.matmul(bank[0:RK, 0:T], wx[:, d, 0:RK], u[:, d, :],
                                       start=(d == 0), stop=(d == DT - 1))
                    mm.then_inc(S["dlr_ps"], 1)
                if slot == 8:
                    pe.wait_ge(S["dlr_ready"], b + 1)
                    for s in range(2):
                        for d in range(DT):
                            mm = pe.matmul(bank[0:3 * NS, s * T:(s + 1) * T], wx3[:, d, s, :, :], u[:, d, :],
                                           start=(d == 0), stop=(d == DT - 1))
                    mm.then_inc(S["bc_ps"], 1)
                if slot == 9:
                    pe.wait_ge(S["bc_hi"], b + 1)
                    for d in range(DT):
                        mm = pe.matmul(bank[:, d * T:(d + 1) * T], wdt[:, d * P:(d + 1) * P], dlr[:, :],
                                       start=True, stop=True)
                    mm.then_inc(S["dt_ps"], 1)

            def sum_states(b, k):
                pe.wait_ge(S["hs_ready"], b * NU + k + 1)
                pe.matmul(PS[:, 7, :], ident, hs[:, k % 2, :, :], start=(k == 0), stop=(k == NU - 1)
                          ).then_inc(S["y_acc"], 1)

            def scans(b, slot):
                if slot in UNIT_AT:
                    k = UNIT_AT[slot]
                    if k == 0:
                        pe.wait_ge(S["bc_ready"], b + 1)
                        if not isinstance(b, int) or b > 0:
                            pe.wait_ge(S["x4_ready"], b)
                    else:
                        pe.wait_ge(S["c_ready"], b * NU + k)
                    for n in range(NQ):
                        mm = pe.matmul(PS[:, 6, n * T:(n + 1) * T], pick_s[:, NQ * k + n, :], bcs[:, 1, :],
                                       start=True, stop=True)
                    mm.then_inc(S["c_ps"], 1)
                    if k > 0:
                        pe.wait_ge(S["dBu_ready"], b * NU + k)
                    for n in range(NQ):
                        mm = pe.matmul(PS[:, 5, n * T:(n + 1) * T], pick_s[:, NQ * k + n, :], bcs[:, 0, :],
                                       start=True, stop=True)
                    mm.then_inc(S["b_ps"], 1)
                    if k > 0:
                        sum_states(b, k - 1)
                if slot == 12:
                    sum_states(b, NU - 1)
                if slot == 13:
                    pe.wait_ge(S["ym_ready"], b + 1)
                    for t in range(TT):
                        for d in range(DT):
                            mm = pe.matmul(PS[:, 5, t * C:(t + 1) * C], ym[:, d, t * P:(t + 1) * P],
                                           wout[:, d, :], start=(d == 0), stop=(d == DT - 1))
                    mm.then_inc(S["out_ps"], 1)
                if slot == 15:
                    pe.wait_ge(S["g_xn_ready"], b + 1)
                    turn(g_xn, PS[:, 6, :], S["g_xT_ps"])
                if slot == 16:
                    pe.wait_ge(S["g_xT_ready"], b + 1)
                    project(g_xT, ffnM[:, :], PS[:, 5, :], S["g_ps"])

            pipeline(pe, (softmaxes, inverse, inner, scans))

        @block.scalar
        def _(act):
            act.preload_act_table_set("natural_log_exp_and_others")

            def copy(dst, src, scale=1.0):
                return act.activation(dst, src, ACT.Copy, scale=scale)

            def first_rstd(b, n):
                act.wait_ge(var_ready[n], b + 1)
                act_link[n](act, act.activation(rs[n][:, 0, :], mv[n][:, :, 1], ACT.Ln, bias=const("eps")))
                act.activation(rs[n][:, 1, :], rs[n][:, 0, :], ACT.Exp, scale=-0.5).then_inc(rs0_ready[n], 1)

            act.wait_ge(S["weights_in"], 16 * NW)
            act.wait_ge(S["tables_in"], 16)
            act.activation(negA[:, :, :], negA[:, :, :], ACT.Exp).then_inc(S["expA"], 1)
            act.wait_ge(S["expA"], 1)
            act.activation(negA[:, :, :], negA[:, :, :], ACT.Copy, scale=-1.0).then_inc(S["negA_ready"], 1)
            act.activation(pick_s[:, :, :], pick_f[:, :].rearrange("p (n m) -> p n m", m=P), ACT.Copy
                           ).then_inc(S["pick_cast"], 1)
            act.wait_ge(S["fT_ps"], 1)
            copy(fT[:, :, :], PS[:, 0, 0:2 * P].rearrange("p (a m) -> p a m", m=P)).then_inc(S["fT_sb"], 1)
            act.wait_ge(S["ffnM_ps"], 1)
            copy(ffnM[:, :], PS[:, 1, 0:P]).then_inc(S["ffnM_sb"], 1)
            act.wait_ge(S["negA_ready"], 1)
            act.wait_ge(S["zeros_ready"], 1)

            def softmaxes(b, slot):
                if slot == 0:
                    act_link[0].start(b)
                    first_rstd(b, 0)
                if slot == 1:
                    act.wait_ge(S["a_xT_ps"], b + 1)
                    copy(a_xT[:, :], PS[:, 0, 0:T]).then_inc(S["a_xT_ready"], 1)
                if slot == 2:
                    act.wait_ge(S["qk_ps"], b + 1)
                    copy(qkT[:, :, :], PS[:, 0, :].rearrange("p (a t) -> p a t", a=2)).then_inc(S["qk_ready"], 1)
                if slot == 5:
                    act.wait_ge(S["K_sub"], 2 * b + 2)
                    act.activation(Ks[:, :, :], Ks[:, :, :], ACT.Exp).then_inc(S["K_exp"], 1)
                if slot in (6, 8):
                    h = (slot - 6) // 2
                    act.wait_ge(S["N_max"], 2 * b + h + 1)
                    for p in range(4):
                        ins = act.activation(EN[:, p, :], PS[:, p // 2, p % 2 * T:(p % 2 + 1) * T], ACT.Exp,
                                             bias=nmaxN[:, 4 * h + p:4 * h + p + 1])
                    ins.then_inc(S["N_exp"], 1)
                if slot in (7, 9):
                    h = (slot - 7) // 2
                    act.wait_ge(S["NT_ps"], 4 * b + 2 * h + 1)
                    copy(ENT[:, 0, 4 * h:4 * h + 4, :], PS[:, 0, :].rearrange("p (q m) -> p q m", m=P)
                         ).then_inc(S["NT_act"], 1)
                if slot in (13, 15):
                    h = (slot - 13) // 2
                    act.wait_ge(S["L_sub"], 2 * b + h + 1)
                    act.activation(EL[:, :, :, :], EL[:, :, :, :], ACT.Exp).then_inc(S["L_exp"], 1)
                if slot in (14, 16):
                    h = (slot - 14) // 2
                    act.wait_ge(S["LT_ps"], 4 * b + 2 * h + 1)
                    copy(ELT[:, 0, 4 * h:4 * h + 4, :], PS[:, 0, :].rearrange("p (q m) -> p q m", m=P)
                         ).then_inc(S["LT_act"], 1)

            def inverse(b, slot):
                j, cube = slot // 2, slot % 2
                if slot == 0:
                    act_link[1].start(b)
                if j < NITER and not cube:
                    for e in range(2):
                        act.wait_ge(S["M_ready"], b * 2 * NITER + 2 * j + e + 1)
                        for s in range(2):
                            h = slice(s * NL, (s + 1) * NL)
                            ins = copy(Abd[h, 4 * e:4 * e + 4, s * NL:(s + 1) * NL],
                                       PS[h, 2 + e, :].rearrange("p (q m) -> p q m", m=P)[:, :, 0:NL], 0.25)
                        ins.then_inc(S["A_bd"], 1)
                if slot == 13:
                    act.wait_ge(S["yT_ps"], b + 1)
                    copy(yT[:, :], PS[:, 3, 0:T]).then_inc(S["yT_ready"], 1)
                if slot == 14:
                    first_rstd(b, 1)
                if slot == 15:
                    act.wait_ge(S["f_xT_ps"], b + 1)
                    copy(f_xT[:, :], PS[:, 3, 0:T]).then_inc(S["f_xT_ready"], 1)

            def inner(b, slot):
                bank, link = PS[:, 4, :], act_link[2]
                if slot == 0:
                    link.start(b)
                    first_rstd(b, 2)
                if slot == 1:
                    act.wait_ge(S["m_xT_ps"], b + 1)
                    copy(xpT[:, KC - 1:KC - 1 + T], bank[:, 0:T]).then_inc(S["m_xT_ready"], 1)
                if slot == 2:
                    act.wait_ge(S["conv_ps"], b + 1)
                    for d in range(DT):
                        ins = act.activation(vr[:, 0, d, :], bank[:, d * T:(d + 1) * T], ACT.Identity,
                                             bias=convb[:, d:d + 1])
                    ins.then_inc(S["conv_out"], 1)
                if slot == 3:
                    act.wait_ge(S["res_ps"], b + 1)
                    copy(vr[:, 1, :, :], bank.rearrange("p (d t) -> p d t", t=T)).then_inc(S["res_out"], 1)
                    act.wait_ge(S["res_out"], b + 1)
                    act.activation(gate[:, :, :, :], vr[:, :, :, :], ACT.Exp, scale=-1.0
                                   ).then_inc(S["gate_exp"], 1)
                if slot == 5:
                    act.wait_ge(S["gate_cut"], b + 1)
                    link(act, act.activation(gate[:, :, :, :], gate[:, :, :, :], ACT.Ln, bias=const("one")))
                    act.activation(gate[:, :, :, :], gate[:, :, :, :], ACT.Exp, scale=-1.0
                                   ).then_inc(S["gate_ready"], 1)
                if slot == 7:
                    act.wait_ge(S["dlr_ps"], b + 1)
                    copy(dlr[:, :], bank[0:RK, 0:T]).then_inc(S["dlr_ready"], 1)
                if slot == 8:
                    act.wait_ge(S["bc_ps"], b + 1)
                    src = bank[0:3 * NS, :].rearrange("p (s t) -> p s t", t=T)
                    copy(bc[:, :, :], src)
                    copy(bch[:, :, :], src).then_inc(S["bc_hi"], 1)
                if slot == 9:
                    act.wait_ge(S["dt_ps"], b + 1)
                    for d in range(DT):
                        ins = act.activation(spa[:, d, :], bank[:, d * T:(d + 1) * T], ACT.Abs,
                                             bias=bdt[:, d:d + 1])
                    ins.then_inc(S["abs_read"], 1)
                if slot == 10:
                    act.wait_ge(S["abs_read"], b + 1)
                    link(act, act.activation(spa[:, :, :], spa[:, :, :], ACT.Exp, scale=-1.0))
                    act.activation(spa[:, :, :], spa[:, :, :], ACT.Ln, bias=const("one")
                                   ).then_inc(S["sp_ready"], 1)

            def scans(b, slot):
                if slot == 0:
                    act_link[3].start(b)
                    act.wait_ge(S["du_ready"], b + 1)
                if slot in UNIT_AT:
                    k = UNIT_AT[slot]
                    if k >= 2:
                        act.wait_ge(S["hs_ready"], b * NU + k - 1)
                    act.wait_ge(S["c_ps"], b * NU + k + 1)
                    copy(c_sb[:, k % 2, :, :], PS[:, 6, :].rearrange("p (n t) -> p n t", t=T)
                         ).then_inc(S["c_ready"], 1)
                    if k >= 2:
                        act.wait_ge(S["h_ready"], b * NU + k - 1)
                    for d in range(DT):
                        for n in range(NQ):
                            ins = act.activation(dA[:, k % 2, d, n, 1:T], delta[:, d, 1:T], ACT.Exp,
                                                 scale=negA[:, d, NQ * k + n:NQ * k + n + 1])
                    ins.then_inc(S["dA_ready"], 1)
                if slot == 13:
                    first_rstd(b, 3)
                if slot == 15:
                    act.wait_ge(S["g_xT_ps"], b + 1)
                    copy(g_xT[:, :], PS[:, 6, 0:T]).then_inc(S["g_xT_ready"], 1)

            pipeline(act, (softmaxes, inverse, inner, scans))

        @block.gpsimd
        def _(pool):
            pool.memset(Abd[:, :, :], 0.0)
            pool.memset(zp[:, :, :], 0.0)
            pool.memset(dA[:, :, :, :, :], 0.0)
            pool.memset(xpT[:, :], 0.0)
            pool.memset(v1[:, :, :, :], 1.0).then_inc(S["filled"], 1)
            pool.wait_ge(S["filled"], 1)
            pool.memset(zp[0:NL, :, HS], 1.0)
            pool.memset(zp[NL:P, :, VC + HS], 1.0).then_inc(S["zeros_ready"], 1)

            def block_diagonal(dst, src):
                n = src.shape[1]
                mask = const("halfones").rearrange("p (s m) -> p s m", m=NL)
                return pool.tensor_tensor(dst.rearrange("p q (s m) -> p q s m", m=NL),
                                          src[:, :, 0:NL].unsqueeze(2).broadcast_to([P, n, 2, NL]),
                                          mask.unsqueeze(1).broadcast_to([P, n, 2, NL]), ALU.mult)

            def biased(b, dst, src, ready, done):
                pool.wait_ge(ready, b + 1)
                pool.tensor_tensor(dst[:, :, :], src[:, :, :], bias_b[:, :].unsqueeze(1).broadcast_to([P, TT, C]),
                                   ALU.add).then_inc(done, 1)

            def softmaxes(b, slot):
                if slot == 8:
                    pool.wait_ge(S["K_ready"], b + 1)
                    block_diagonal(Kbd[:, :, :], Ks[:, :, :]).then_inc(S["Kbd_ready"], 1)
                if slot == 11:
                    pool.wait_ge(S["Y_ready"], b + 1)
                    for e in range(2):
                        block_diagonal(Ybd[:, 4 * e:4 * e + 4, :], Yz[:, 4 * e:4 * e + 4, :]
                                       ).then_inc(S["Ybd_ready"], 1)

            def inverse(b, slot):
                j, cube = slot // 2, slot % 2
                if j < NITER - 1 and cube:
                    for e in range(2):
                        pool.wait_ge(S["YZ_ready"], b * 2 * (NITER - 1) + 2 * j + e + 1)
                        block_diagonal(Ybd[:, 4 * e:4 * e + 4, :], Yz[:, 4 * e:4 * e + 4, :]
                                       ).then_inc(S["Ybd_ready"], 1)
                if slot == 14:
                    biased(b, x1b, x1, S["x1_ready"], S["x1b_ready"])

            def inner(b, slot):
                if slot == 12:
                    pool.wait_ge(S["delta_ready"], b + 1)
                    pool.tensor_tensor(du[:, :, :], delta[:, :, :], u[:, :, :], ALU.mult
                                       ).then_inc(S["du_ready"], 1)

            def scans(b, slot):
                if slot in UNIT_AT:
                    k = UNIT_AT[slot]
                    pool.wait_ge(S["h_ready"], b * NU + k + 1)
                    pool.wait_ge(S["c_ready"], b * NU + k + 1)
                    pool.tensor_tensor(hc[:, :, :, :].rearrange("p d n t -> p d (n t)"),
                                       hst[:, k % 2, :, :, :].rearrange("p d n t -> p d (n t)"),
                                       c_sb[:, k % 2, :, :].rearrange("p n t -> p (n t)").unsqueeze(1)
                                       .broadcast_to([P, DT, NQ * T]), ALU.mult).then_inc(S["hc_ready"], 1)
                    pool.wait_ge(S["hc_ready"], b * NU + k + 1)
                    if k >= 2:
                        pool.wait_ge(S["y_acc"], b * NU + k - 1)
                    pool.tensor_tensor(hs[:, k % 2, :, :], hc[:, :, 0, :], hc[:, :, 1, :], ALU.add
                                       ).then_inc(S["hs_ready"], 1)
                    pool.wait_ge(S["hs_ready"], b * NU + k + 1)
                if slot == 13:
                    biased(b, x3b, x3, S["x3_ready"], S["x3b_ready"])

            pool.wait_ge(S["weights_in"], 16 * NW)
            pool.wait_ge(S["tables_in"], 16)
            pipeline(pool, (softmaxes, inverse, inner, scans))

        @block.vector
        def _(dve):
            dve.wait_ge(S["weights_in"], 16 * NW)
            dve.wait_ge(S["tables_in"], 16)
            dve.tensor_tensor(wconv[:, :, :], convw_b[:, :, :],
                              win[:, 0:DI].unsqueeze(1).broadcast_to([P, KC, DI]), ALU.mult
                              ).then_inc(S["convw_ready"], 1)
            for s in range(2):
                for r in range(3):
                    ins = dve.tensor_copy(wx3[:, :, s, r, :], wx[:, :, RK + s * NS:RK + (s + 1) * NS])
            ins.then_inc(S["wx3_ready"], 1)
            dve.wait_ge(S["zeros_ready"], 1)

            def statistics(n, src):
                for t in range(TT):
                    ins = dve.bn_stats(st[n][:, t, :], src[:, t, :])
                dve_link[n](dve, ins)
                dve.memset(pause[:, :], 0.0)
                for t in range(TT):
                    ins = dve.bn_aggr(mv[n][:, t, :], st[n][:, t, :])
                ins.then_inc(var_ready[n], 1)

            def normalise(b, n, src, dst, done):
                link, r = dve_link[n], rs[n]
                dve.wait_ge(rs0_ready[n], b + 1)
                link(dve, dve.tensor_tensor(r[:, 2, :], r[:, 1, :], r[:, 1, :], ALU.mult))
                link(dve, dve.scalar_tensor_tensor(out=r[:, 3, :], in0=mv[n][:, :, 1], scalar=EPS,
                                                   in1=r[:, 2, :], op0=ALU.add, op1=ALU.mult))
                link(dve, dve.tensor_scalar(r[:, 2, :], r[:, 3, :], -0.5, 1.5, ALU.mult, ALU.add))
                link(dve, dve.tensor_tensor(r[:, 3, :], r[:, 2, :], r[:, 1, :], ALU.mult))
                for t in range(TT):
                    ins = dve.tensor_scalar(dst[:, t, :], src[:, t, :], mv[n][:, t, 0:1], r[:, 3, t:t + 1],
                                            ALU.subtract, ALU.mult)
                ins.then_inc(done, 1)

            def spread(ap, n):
                return ap.unsqueeze(2).broadcast_to([ap.shape[0], ap.shape[1], n])

            def add_rows(dst, src, bank, done):
                dve.tensor_tensor(dst[:, :, :], src[:, :, :], bank[:, 0:T].rearrange("p (t c) -> p t c", c=C),
                                  ALU.add).then_inc(done, 1)

            def softmaxes(b, slot):
                link = dve_link[0]
                if slot == 0:
                    link.start(b)
                    dve.wait_ge(S["x_in"], 16 * b + 16)
                    statistics(0, xin)
                if slot == 1:
                    normalise(b, 0, xin, a_xn, S["a_xn_ready"])
                if slot == 2:
                    dve.wait_ge(S["v_ps"], b + 1)
                    dve.tensor_copy(v1[:, :, :, 0:HS].rearrange("p t h d -> p (t h) d"),
                                    PS[:, 1, 0:T].rearrange("p (t d) -> p t d", d=HS)
                                    ).then_inc(S["v_ready"], 1)
                if slot == 3:
                    dve.wait_ge(S["qk_ready"], b + 1)
                    link(dve, dve.tensor_reduce(lm[:, :, :].rearrange("p a l -> p (a l)"),
                                                qkT[:, :, :].rearrange("p a (l r) -> p (a l) r", r=POOLED),
                                                AX.X, ALU.add))
                    dve.tensor_tensor(qz[:, :, :], lm[:, 0, :].unsqueeze(1).broadcast_to([P, 4, NL]),
                                      spread(const("headmask"), NL), ALU.mult)
                    dve.tensor_scalar(klu[:, :], lm[:, 1, :], 1.0 / POOLED, None, ALU.mult)
                    dve.tensor_tensor(kz[:, :, :], lm[:, 1, :].unsqueeze(1).broadcast_to([P, 4, NL]),
                                      spread(const("headmask"), NL), ALU.mult).then_inc(S["lm_ready"], 1)
                if slot in (4, 5):
                    h = slot - 4
                    dve.wait_ge(S["K_ps"], 2 * b + h + 1)
                    sc = PS[:, 0:2, 0:2 * NL].rearrange("p g (j m) -> p g j m", m=NL)
                    mx = nmaxK[:, 4 * h:4 * h + 4].rearrange("p (g j) -> p g j", j=2)
                    link(dve, dve.tensor_reduce(mx, sc, AX.X, ALU.max, negate=True))
                    dve.tensor_tensor(Ks[:, 4 * h:4 * h + 4, :].rearrange("p (g j) m -> p g j m", j=2), sc,
                                      mx.unsqueeze(3).broadcast_to([P, 2, 2, NL]), ALU.add
                                      ).then_inc(S["K_sub"], 1)
                if slot in (6, 8):
                    h = (slot - 6) // 2
                    dve.wait_ge(S["N_ps"], 2 * b + h + 1)
                    dve.tensor_reduce(nmaxN[:, 4 * h:4 * h + 4],
                                      PS[:, 0:2, :].rearrange("p g (j t) -> p (g j) t", t=T),
                                      AX.X, ALU.max, negate=True).then_inc(S["N_max"], 1)
                if slot == 6:
                    dve.wait_ge(S["K_exp"], b + 1)
                    link(dve, dve.tensor_reduce(sumK[:, :], Ks[:, :, :], AX.X, ALU.add))
                    link(dve, dve.reciprocal(rsumK[:, :], sumK[:, :]))
                    dve.tensor_tensor(Ks[:, :, :], Ks[:, :, :], spread(rsumK[:, :], NL), ALU.mult
                                      ).then_inc(S["K_ready"], 1)
                if slot in (7, 9):
                    h = (slot - 7) // 2
                    dve.wait_ge(S["NT_ps"], 4 * b + 2 * h + 2)
                    dve.tensor_copy(ENT[:, 1, 4 * h:4 * h + 4, :], PS[:, 1, :].rearrange("p (q m) -> p q m", m=P)
                                    ).then_inc(S["NT_dve"], 1)
                if slot == 10:
                    dve.wait_ge(S["nv_ps"], b + 1)
                    nv = PS[:, 0, 0:NP * 2 * VC].rearrange("p (q c) -> p q c", c=2 * VC)
                    for s in range(2):
                        h = slice(s * NL, (s + 1) * NL)
                        ins = dve.reciprocal(rsumN[h, :], nv[h, :, s * VC + HS])
                    link(dve, ins)
                    for s in range(2):
                        h = slice(s * NL, (s + 1) * NL)
                        ins = dve.tensor_tensor(wv[h, :, :], nv[h, :, s * VC:s * VC + HS],
                                                spread(rsumN[h, :], HS), ALU.mult)
                    ins.then_inc(S["w_ready"], 1)
                if slot == 11:
                    dve.wait_ge(S["cy_ps"], b + 1)
                    link(dve, dve.tensor_reduce(den[:, :], PS[:, 1, :].rearrange("p (q m) -> p q m", m=NL),
                                                AX.X, ALU.max))
                    link(dve, dve.reciprocal(rden[:, :], den[:, :]))
                    dve.tensor_tensor(Yz[:, :, 0:NL], PS[:, 0, :].rearrange("p (q m) -> p q m", m=NL),
                                      spread(rden[:, :], NL), ALU.mult).then_inc(S["Y_ready"], 1)
                if slot == 12:
                    dve.wait_ge(S["z0_ps"], b + 1)
                    dve.tensor_tensor(Yz[:, :, NL:ZC], PS[:, 1, 0:NP * HS].rearrange("p (q c) -> p q c", c=HS),
                                      spread(rden[:, :], HS), ALU.mult).then_inc(S["z_ready"], 1)
                if slot in (13, 15):
                    h = (slot - 13) // 2
                    dve.wait_ge(S["L_ps"], 2 * b + h + 1)
                    flat = PS[:, 0:2, :].rearrange("p a (j m) -> p (a j) m", m=NL)
                    link(dve, dve.tensor_reduce(nmaxL[:, :], flat, AX.X, ALU.max, negate=True))
                    dve.tensor_tensor(EL[:, :, :, :].rearrange("p g t (j m) -> p (g t j) m", m=NL), flat,
                                      spread(nmaxL[:, :], NL), ALU.add).then_inc(S["L_sub"], 1)
                if slot in (14, 16):
                    h = (slot - 14) // 2
                    dve.wait_ge(S["LT_ps"], 4 * b + 2 * h + 2)
                    dve.tensor_copy(ELT[:, 1, 4 * h:4 * h + 4, :], PS[:, 1, :].rearrange("p (q m) -> p q m", m=P)
                                    ).then_inc(S["LT_dve"], 1)

            def inverse(b, slot):
                j, cube, last = slot // 2, slot % 2, slot // 2 == NITER - 1
                c0 = NL if last else 0
                if slot == 0:
                    dve_link[1].start(b)
                    dve.wait_ge(S["z_ready"], b + 1)
                if j < NITER and not cube:
                    for e in range(2):
                        dve.wait_ge(S["sq_ps"], b * 2 * NITER + 2 * j + e + 1)
                        if j > 0:
                            dve.wait_ge(S["YZ_ready"], b * 2 * (NITER - 1) + 2 * j)
                        q = slice(4 * e, 4 * e + 4)
                        au = PS[:, 2 + e, :].rearrange("p (q m) -> p q m", m=P)[:, :, c0:ZC]
                        dve.scalar_tensor_tensor(out=Hz[:, q, c0:ZC], in0=au, scalar=-15.0 / 13.0,
                                                 in1=Yz[:, q, c0:ZC], op0=ALU.mult, op1=ALU.add)
                        dve.scalar_tensor_tensor(out=Mr[:, q, c0:ZC], in0=Yz[:, q, c0:ZC], scalar=-7.0,
                                                 in1=au, op0=ALU.mult, op1=ALU.add
                                                 ).then_inc(S["M_ready"], 1)
                if j < NITER and cube:
                    for e in range(2):
                        dve.wait_ge(S["cube_ps"], b * 2 * NITER + 2 * j + e + 1)
                        q = slice(4 * e, 4 * e + 4)
                        cu = PS[:, 2 + e, :].rearrange("p (q m) -> p q m", m=P)
                        if last:
                            for s in range(2):
                                h = slice(s * NL, (s + 1) * NL)
                                ins = dve.scalar_tensor_tensor(out=zp[h, q, s * VC:s * VC + HS],
                                                               in0=Hz[h, q, NL:ZC], scalar=3.25,
                                                               in1=cu[h, :, NL:ZC], op0=ALU.mult,
                                                               op1=ALU.subtract)
                            if e == 1:
                                ins.then_inc(S["zp_ready"], 1)
                        else:
                            dve.scalar_tensor_tensor(out=Yz[:, q, :], in0=Hz[:, q, :], scalar=3.25,
                                                     in1=cu[:, :, 0:ZC], op0=ALU.mult, op1=ALU.subtract
                                                     ).then_inc(S["YZ_ready"], 1)
                if slot == 12:
                    dve.wait_ge(S["y_ps"], b + 1)
                    yp = PS[:, 2, 0:TT * NH * VC].rearrange("p (t c) -> p t c", c=VC)
                    dve_link[1](dve, dve.reciprocal(rsumL[:, :], yp[:, :, HS]))
                    dve.tensor_tensor(yat[:, :, :, :].rearrange("p t h d -> p (t h) d"), yp[:, :, 0:HS],
                                      spread(rsumL[:, :], HS), ALU.mult).then_inc(S["y_ready"], 1)
                if slot == 14:
                    dve.wait_ge(S["proj_ps"], b + 1)
                    dve.wait_ge(S["xres_in"], 16 * b + 16)
                    add_rows(x1, xres, PS[:, 2, :], S["x1_ready"])
                    dve.wait_ge(S["x1_ready"], b + 1)
                    statistics(1, x1)
                if slot == 15:
                    normalise(b, 1, x1, f_xn, S["f_xn_ready"])
                if slot == 16:
                    dve.wait_ge(S["f_ps"], b + 1)
                    dve.wait_ge(S["x1b_ready"], b + 1)
                    add_rows(x2, x1b, PS[:, 2, :], S["x2_ready"])

            def inner(b, slot):
                bank, link = PS[:, 4, :], dve_link[2]
                if slot == 0:
                    link.start(b)
                    dve.wait_ge(S["x2_ready"], b + 1)
                    statistics(2, x2)
                if slot == 1:
                    normalise(b, 2, x2, m_xn, S["m_xn_ready"])
                if slot == 4:
                    dve.wait_ge(S["gate_exp"], b + 1)
                    dve.tensor_scalar(gate[:, :, :, :], gate[:, :, :, :], LN_MOST, None, ALU.min
                                      ).then_inc(S["gate_cut"], 1)
                if slot == 6:
                    dve.wait_ge(S["gate_ready"], b + 1)
                    dve.tensor_tensor(u[:, :, :], vr[:, 0, :, :], gate[:, 0, :, :], ALU.mult
                                      ).then_inc(S["u_ready"], 1)
                if slot == 9:
                    dve.wait_ge(S["bc_hi"], b + 1)
                    link(dve, dve.scalar_tensor_tensor(out=bc[:, :, :], in0=bch[:, :, :],
                                                       scalar=const("part1")[0:3 * NS, :], in1=bc[:, :, :],
                                                       op0=ALU.mult, op1=ALU.add))
                    link(dve, dve.tensor_copy(bch[:, :, :], bc[:, :, :]))
                if slot == 10:
                    dve.wait_ge(S["abs_read"], b + 1)
                    for d in range(DT):
                        ins = dve.tensor_scalar(spp[:, d, :], bank[:, d * T:(d + 1) * T], bdt[:, d:d + 1], 0.0,
                                                ALU.add, ALU.max)
                    link(dve, ins)
                if slot == 12:
                    dve.scalar_tensor_tensor(out=bcs[:, :, :], in0=bch[:, :, :],
                                             scalar=const("part2")[0:3 * NS, :], in1=bc[:, :, :],
                                             op0=ALU.mult, op1=ALU.add).then_inc(S["bc_ready"], 1)
                    dve.wait_ge(S["sp_ready"], b + 1)
                    dve.tensor_tensor(delta[:, :, :], spp[:, :, :], spa[:, :, :], ALU.add
                                      ).then_inc(S["delta_ready"], 1)
                if slot == 13:
                    if not isinstance(b, int) or b > 0:
                        dve.wait_ge(S["ym_ready"], b)
                    for d in range(DT):
                        dve.tensor_scalar(uD[:, d, :], u[:, d, :], dskip[:, d:d + 1], None, ALU.mult)
                    dve.tensor_tensor(sres[:, :, :], vr[:, 1, :, :], gate[:, 1, :, :], ALU.mult
                                      ).then_inc(S["sres_ready"], 1)
                if slot == 14:
                    if not isinstance(b, int) or b > 0:
                        dve.wait_ge(S["x3_ready"], b)
                    dve.tensor_copy(x2b[:, :, :], x2[:, :, :]).then_inc(S["x2b_ready"], 1)
                    dve.wait_ge(S["x2b_ready"], b + 1)

            def scans(b, slot):
                link = dve_link[3]
                if slot == 0:
                    link.start(b)
                    dve.wait_ge(S["du_ready"], b + 1)
                if slot in UNIT_AT:
                    k = UNIT_AT[slot]
                    dve.wait_ge(S["b_ps"], b * NU + k + 1)
                    if k >= 2:
                        dve.wait_ge(S["h_ready"], b * NU + k - 1)
                    dve.tensor_tensor(dBu[:, k % 2, :, :, :],
                                      PS[:, 5, :].rearrange("p (n t) -> p n t", t=T).unsqueeze(1)
                                      .broadcast_to([P, DT, NQ, T]),
                                      du[:, :, :].unsqueeze(2).broadcast_to([P, DT, NQ, T]), ALU.mult
                                      ).then_inc(S["dBu_ready"], 1)
                    dve.wait_ge(S["dBu_ready"], b * NU + k + 1)
                    dve.wait_ge(S["dA_ready"], b * NU + k + 1)
                    if k >= 2:
                        dve.wait_ge(S["hs_ready"], b * NU + k - 1)
                    dve.tensor_tensor_scan(hst[:, k % 2, :, :, :].rearrange("p d n t -> p (d n t)"),
                                           dA[:, k % 2, :, :, :].rearrange("p d n t -> p (d n t)"),
                                           dBu[:, k % 2, :, :, :].rearrange("p d n t -> p (d n t)"),
                                           0.0, ALU.mult, ALU.add).then_inc(S["h_ready"], 1)
                if slot == 12:
                    dve.wait_ge(S["y_acc"], b * NU + NU)
                    dve.wait_ge(S["sres_ready"], b + 1)
                    link(dve, dve.tensor_tensor(ysum[:, :, :], uD[:, :, :],
                                                PS[:, 7, :].rearrange("p (d t) -> p d t", t=T), ALU.add))
                    dve.tensor_tensor(ym[:, :, :], ysum[:, :, :], sres[:, :, :], ALU.mult
                                      ).then_inc(S["ym_ready"], 1)
                if slot == 13:
                    dve.wait_ge(S["out_ps"], b + 1)
                    add_rows(x3, x2b, PS[:, 5, :], S["x3_ready"])
                    dve.wait_ge(S["x3_ready"], b + 1)
                    statistics(3, x3)
                if slot == 14:
                    normalise(b, 3, x3, g_xn, S["g_xn_ready"])
                if slot == 16:
                    dve.wait_ge(S["g_ps"], b + 1)
                    dve.wait_ge(S["x3b_ready"], b + 1)
                    if isinstance(b, int) and b > 0:
                        dve.wait_ge(S["x_out"], 16 * b)
                    add_rows(x4, x3b, PS[:, 5, :], S["x4_ready"])

            pipeline(dve, (softmaxes, inverse, inner, scans))


_INS = ['L0_attn_a_x', 'L0_attn_a_W_attn', 'L0_attn_a_W_proj', 'L0_attn_b_W_in', 'L0_attn_b_conv_w',
        'L0_attn_b_conv_b', 'L0_attn_b_W_x', 'L0_attn_b_W_dt', 'L0_attn_b_b_dt', 'L0_attn_b_A_log',
        'L0_attn_b_D', 'L0_attn_b_W_out', 'L0_ffn_w_freq_real', 'L0_ffn_w_freq_imag', 'L0_ffn_bias']


def kernel(**inputs):
    import numpy as _np
    import concourse.bacc as _bacc
    from concourse import mybir as _mybir
    from concourse.bass_utils import run_bass_kernel_spmd as _run

    nc = _bacc.Bacc("TRN2", target_bir_lowering=False, num_devices=1)
    tab, pick = shape_tables()
    arrays, args = {}, []
    for name, a in [(n, inputs[n]) for n in _INS] + [("tab", tab), ("pick", pick)]:
        a = _np.ascontiguousarray(a)
        arrays[f"in_{name}"] = a
        args.append(nc.dram_tensor(f"in_{name}", a.shape, _mybir.dt.from_np(a.dtype), kind="ExternalInput").ap())
    args.append(nc.dram_tensor("out_x", (B, T, C), F32, kind="ExternalOutput").ap())
    hybrid_layer_kernel(nc, *args)
    r = _run(nc, [arrays], core_ids=[0])
    return r.results[0]["out_x"]
```

```python
from contextlib import ExitStack

import numpy as np

import concourse.bass as bass
from concourse import mybir

F32 = mybir.dt.float32
BF16 = mybir.dt.bfloat16
ALU = mybir.AluOpType
ACT = mybir.ActivationFunctionType
AX = mybir.AxisListType

P = 128
B, T, C = 16, 256, 128
TT = T // P
NH, HS, NL = 16, 8, 64
NP = NH // 2
POOLED = T // NL
NITER = 6
ZC = NL + HS
VC = HS + 1
DI, DT = 256, 2
NS, RK, KC = 16, 64, 4
NQ = 2
NU = NS // NQ
WIDE = 7
SLOTS = 18
UNIT_AT = {0: 0, 1: 1, 2: 2, 4: 3, 5: 4, 7: 5, 8: 6, 10: 7}
DVE_LINKS = (5, 6, 7, 5, 7)
ACT_LINKS = (1, 1, 3, 1)
EPS = 1e-5
YS = 1.75 ** 0.5
LN_MOST = 2.0 ** 62

TAB = {}
_at = 0
for _name, _n in (("ident", P), ("halfsum", P), ("cos", P), ("sin", P), ("nsin", P), ("icos", P),
                  ("insin", P), ("headmask", NH), ("part1", 1), ("part2", 1), ("eps", 1), ("one", 1)):
    TAB[_name] = (_at, _at + _n)
    _at += _n
TABW = _at


def shape_tables():
    tab = np.zeros((P, TABW), np.float32)
    p = np.arange(P)
    angle = 2 * np.pi * (np.outer(p, p) % C) / C

    def put(name, a):
        tab[:, TAB[name][0]:TAB[name][1]] = a
    put("ident", np.eye(P))
    put("halfsum", (p[:, None] // NL == p[None, :] // NL) / YS)
    put("cos", np.cos(angle))
    put("sin", np.sin(angle))
    put("nsin", -np.sin(angle))
    put("icos", np.cos(angle) / C)
    put("insin", -np.sin(angle) / C)
    put("headmask", (p[:, None] // HS == np.arange(NH)[None, :]) / POOLED)
    put("part1", -(p[:, None] // NS >= 1).astype(np.float32))
    put("part2", -(p[:, None] // NS >= 2).astype(np.float32))
    put("eps", EPS)
    put("one", 1.0)
    pick = np.zeros((3 * NS, NS, P), np.float32)
    for r in range(3 * NS):
        pick[r, r % NS, :] = 1.0
    return tab, pick.reshape(3 * NS, NS * P)


class Link:

    def __init__(self, sem, per_batch):
        self.sem, self.per_batch = sem, per_batch

    def start(self, b):
        self.base, self.n = b * self.per_batch, 0

    def __call__(self, eng, ins):
        self.n += 1
        ins.then_inc(self.sem, 1)
        eng.wait_ge(self.sem, self.base + self.n)


def hybrid_layer_kernel(nc, x, W_attn, W_proj, W_in, conv_w, conv_b, W_x, W_dt, b_dt, A_log, D, W_out,
                        w_re, w_im, bias, tab, pick, out):
    ctx = ExitStack()
    with ctx:
        def sb(name, shape, dt=F32):
            return ctx.enter_context(nc.sbuf_tensor(name, shape, dt))

        def sem(name):
            return ctx.enter_context(nc.semaphore(name))

        tb = sb("tb", [P, TABW])
        pick_f = sb("pick_f", [3 * NS, NS * P])
        pick_s = sb("pick_s", [P, NS, P], BF16)
        wqkv = sb("wqkv", [P, 3 * C])
        wproj = sb("wproj", [P, C])
        win = sb("win", [P, 2 * DI])
        convw_b = sb("convw_b", [P, KC, DI])
        wconv = sb("wconv", [P, KC, DI])
        convb = sb("convb", [P, DT])
        wx = sb("wx", [P, DT, RK + 2 * NS])
        wx3 = sb("wx3", [P, DT, 2, 3, NS])
        wdt = sb("wdt", [RK, DI])
        bdt = sb("bdt", [P, DT])
        negA = sb("negA", [P, DT, NS])
        dskip = sb("dskip", [P, DT])
        wout = sb("wout", [P, DT, C])
        wre = sb("wre", [P, P])
        wim = sb("wim", [P, P])
        fT = sb("fT", [P, 2, P])
        ffnM = sb("ffnM", [P, P])
        bias_b = sb("bias_b", [P, C])

        def const(name):
            return tb[:, TAB[name][0]:TAB[name][1]]
        ident = const("ident")

        xin = sb("xin", [P, TT, C])
        a_xn = sb("a_xn", [P, TT, C])
        a_xT = sb("a_xT", [P, T])
        qkT = sb("qkT", [P, 2, T])
        v1 = sb("v1", [P, TT, NH, VC])
        lm = sb("lm", [P, 2, NL])
        qz = sb("qz", [P, NH, NL])
        kz = sb("kz", [P, NH, NL])
        klu = sb("klu", [P, NL])
        nmaxL = sb("nmaxL", [P, TT * NH // 2])
        EL = sb("EL", [P, TT, 8, NL])
        nmaxN = sb("nmaxN", [P, NP])
        EN = sb("EN", [P, 4, T])
        ENT = sb("ENT", [P, TT, NP, P])
        nmaxK = sb("nmaxK", [P, NP])
        Kw = sb("Kw", [P, NP, ZC])
        sumK = sb("sumK", [P, NP])
        rsumK = sb("rsumK", [P, NP])
        den = sb("den", [P, NP])
        rden = sb("rden", [P, NP])
        rsumN = sb("rsumN", [P, NP])
        ELT = sb("ELT", [P, TT, NP, P])
        Yz = sb("Yz", [P, NP, ZC])

        xres = sb("xres", [P, TT, C])
        Hz = sb("Hz", [P, NP, ZC])
        Mr = sb("Mr", [P, NP, ZC])
        Az = sb("Az", [P, NP, ZC])
        zp = sb("zp", [P, NP, 2 * VC])
        rsumL = sb("rsumL", [P, TT * NH])
        yat = sb("yat", [P, TT, NH, HS])
        yT = sb("yT", [P, T])
        x1 = sb("x1", [P, TT, C])
        x1b = sb("x1b", [P, TT, C])
        f_xn = sb("f_xn", [P, TT, C])
        f_xT = sb("f_xT", [P, T])
        x2 = sb("x2", [P, TT, C])

        m_xn = sb("m_xn", [P, TT, C])
        xpT = sb("xpT", [P, KC - 1 + T])
        vr = sb("vr", [P, 2, DT, T])
        gate = sb("gate", [P, 2, DT, T])
        u = sb("u", [P, DT, T])
        dlr = sb("dlr", [RK, T])
        bc = sb("bc", [3 * NS, 2, T])
        bch = sb("bch", [3 * NS, 2, T], BF16)
        spa = sb("spa", [P, DT, T])
        spp = sb("spp", [P, DT, T])
        delta = sb("delta", [P, DT, T])
        du = sb("du", [P, DT, T])
        bcs = sb("bcs", [P, 2, T], BF16)
        uD = sb("uD", [P, DT, T])
        sres = sb("sres", [P, DT, T])
        x2b = sb("x2b", [P, TT, C])

        c_sb = sb("c_sb", [P, 2, NQ, T])
        dA = sb("dA", [P, 2, DT, NQ, T])
        dBu = sb("dBu", [P, 2, DT, NQ, T])
        hst = sb("hst", [P, 2, DT, NQ, T])
        hc = sb("hc", [P, DT, NQ, T])
        hs = sb("hs", [P, 2, DT, T])
        ysum = sb("ysum", [P, DT, T])
        ym = sb("ym", [P, DT, T])
        x3 = sb("x3", [P, TT, C])
        x3b = sb("x3b", [P, TT, C])
        g_xn = sb("g_xn", [P, TT, C])
        g_xT = sb("g_xT", [P, T])
        x4 = sb("x4", [P, TT, C])

        pause = sb("pause", [P, 1])
        st = [sb(f"st{n}", [P, TT, 6]) for n in range(4)]
        mv = [sb(f"mv{n}", [P, TT, 2]) for n in range(4)]
        rs = [sb(f"rs{n}", [P, 4, TT]) for n in range(4)]

        PS = ctx.enter_context(nc.psum_tensor("PS", [P, 7, 512], F32))

        names = """weights_in tables_in x_in xres_in x_out
            pick_cast expA negA_ready convw_ready wx3_ready filled zeros_ready fT_ps fT_sb ffnM_ps ffnM_sb
            a_xn_ready a_xT_ps a_xT_ready v_ps v_ready qk_ps qk_ready qz_ready kz_ready lm_ready
            K_ps K_sub K_exp K_ready N_ps N_max N_exp NT_ps NT_act NT_dve nv_ps w_ready
            cs_ps Y0_ps YZ_ready L_ps L_sub L_exp LT_ps LT_act LT_dve
            heads_go sq_ps A_ready M_ready H_ready cube_ps zp_ready
            y_ps y_ready yT_ps yT_ready proj_ps x1_ready x1b_ready f_xn_ready f_xT_ps f_xT_ready f_ps x2_ready
            m_xn_ready m_xT_ps m_xT_ready conv_ps conv_out res_ps res_out gate_exp gate_cut gate_ready u_ready
            dlr_ps dlr_ready bc_ps bc_hi bc_ready dt_ps abs_read max_ready sp_ready delta_ready du_ready uD_ready sres_ready x2b_ready
            b_ps c_ps c_ready dA_ready dBu_ready h_ready hc_ready hs_ready y_acc ym_ready out_ps x3_ready x3b_ready
            g_xn_ready g_xT_ps g_xT_ready g_ps x4_ready""".split()
        S = {n: sem(n) for n in names}
        var_ready = [sem(f"var_ready{n}") for n in range(4)]
        rs0_ready = [sem(f"rs0_ready{n}") for n in range(4)]
        dve_link = [Link(sem(f"dve_link{n}"), k) for n, k in enumerate(DVE_LINKS)]
        act_link = [Link(sem(f"act_link{n}"), k) for n, k in enumerate(ACT_LINKS)]
        NW = 15

        block = ctx.enter_context(nc.Block())

        def pipeline(eng, *stages):
            def turn_of_loop(i, lowest, highest):
                for slot in range(SLOTS):
                    for n, stage in stages:
                        if lowest <= n <= highest:
                            stage(i - n, slot)
            for i in range(-1, 3):
                turn_of_loop(i, -1, i)
            with eng.Fori(3, B - 1) as i:
                turn_of_loop(i, -1, 3)
            for i in range(B - 1, B + 3):
                turn_of_loop(i, i - B + 1, 3)

        def pairs(bank):
            return PS[:, bank:bank + 2, :].rearrange("p e (q m) -> p (e q) m", m=P)

        @block.sync
        def _(sp):
            def tokens(ap, b):
                return ap[bass.ds(b, 1), :, :].rearrange("b (t p) c -> p (b t) c", p=P)

            def load_x(b):
                sp.dma_start(xin[:, :, :], tokens(x, b)).then_inc(S["x_in"], 16)

            def load_residual(b):
                sp.dma_start(xres[:, :, :], tokens(x, b)).then_inc(S["xres_in"], 16)

            def store(b):
                sp.wait_ge(S["x4_ready"], b + 1)
                sp.dma_start(tokens(out, b), x4[:, :, :]).then_inc(S["x_out"], 16)

            sp.dma_start(tb[:, :], tab).then_inc(S["tables_in"], 16)
            load_x(0)
            sp.dma_start(wqkv[:, :], W_attn).then_inc(S["weights_in"], 16)
            sp.dma_start(wproj[:, :], W_proj).then_inc(S["weights_in"], 16)
            sp.dma_start(wre[:, :], w_re).then_inc(S["weights_in"], 16)
            sp.dma_start(wim[:, :], w_im).then_inc(S["weights_in"], 16)
            sp.dma_start(win[:, :], W_in).then_inc(S["weights_in"], 16)
            sp.dma_start(convw_b[:, :, :], conv_w.rearrange("k a d -> a k d").broadcast_to([P, KC, DI])
                         ).then_inc(S["weights_in"], 16)
            sp.dma_start(convb[:, :], conv_b.rearrange("(t p) -> p t", p=P),
                         allow_slow_non_contiguous=True).then_inc(S["weights_in"], 16)
            sp.dma_start(wx[:, :, :], W_x.rearrange("(t p) r -> p t r", p=P)).then_inc(S["weights_in"], 16)
            sp.dma_start(wdt[:, :], W_dt).then_inc(S["weights_in"], 16)
            sp.dma_start(bdt[:, :], b_dt.rearrange("(t p) -> p t", p=P),
                         allow_slow_non_contiguous=True).then_inc(S["weights_in"], 16)
            sp.dma_start(negA[:, :, :], A_log.rearrange("(t p) n -> p t n", p=P)).then_inc(S["weights_in"], 16)
            sp.dma_start(dskip[:, :], D.rearrange("(t p) -> p t", p=P),
                         allow_slow_non_contiguous=True).then_inc(S["weights_in"], 16)
            sp.dma_start(wout[:, :, :], W_out.rearrange("(t p) c -> p t c", p=P)).then_inc(S["weights_in"], 16)
            sp.dma_start(bias_b[:, :], bias.rearrange("(a c) -> a c", a=1).broadcast_to([P, C])
                         ).then_inc(S["weights_in"], 16)
            sp.dma_start(pick_f[:, :], pick).then_inc(S["weights_in"], 16)

            def turn_of_loop(i, with_store):
                if not isinstance(i, int) or i < B + 1:
                    if not isinstance(i, int) or i > 1:
                        sp.wait_ge(S["x1_ready"], i - 1)
                    if not isinstance(i, int) or i > 3:
                        sp.wait_ge(S["x_out"], 16 * (i - 3))
                    if not isinstance(i, int) or i > 0:
                        load_residual(i - 1)
                if not isinstance(i, int) or i < B - 1:
                    sp.wait_ge(S["a_xn_ready"], i + 1)
                    load_x(i + 1)
                if with_store:
                    store(i - 3)

            for i in range(4):
                turn_of_loop(i, i == 3)
            with sp.Fori(4, B - 1) as i:
                turn_of_loop(i, True)
            for i in range(B - 1, B + 3):
                turn_of_loop(i, True)
            sp.wait_ge(S["x_out"], 16 * B)

        @block.tensor
        def _(pe):
            pe.wait_ge(S["tables_in"], 16)
            pe.wait_ge(S["weights_in"], 16 * NW)
            pe.matmul(PS[:, 0, 0:P], wre[:, :], const("cos"), start=True, stop=False)
            pe.matmul(PS[:, 0, 0:P], wim[:, :], const("sin"), start=False, stop=True)
            pe.matmul(PS[:, 0, P:2 * P], wim[:, :], const("cos"), start=True, stop=False)
            pe.matmul(PS[:, 0, P:2 * P], wre[:, :], const("nsin"), start=False, stop=True
                      ).then_inc(S["fT_ps"], 1)
            pe.wait_ge(S["fT_sb"], 1)
            pe.matmul(PS[:, 1, 0:P], fT[:, 0, :], const("icos"), start=True, stop=False)
            pe.matmul(PS[:, 1, 0:P], fT[:, 1, :], const("insin"), start=False, stop=True
                      ).then_inc(S["ffnM_ps"], 1)
            pe.wait_ge(S["ffnM_sb"], 1)
            pe.wait_ge(S["pick_cast"], 1)
            pe.wait_ge(S["convw_ready"], 1)
            pe.wait_ge(S["wx3_ready"], 1)
            pe.wait_ge(S["zeros_ready"], 1)

            def turn(src, bank, done):
                for t in range(TT):
                    mm = pe.transpose(bank[:, t * P:(t + 1) * P], src[:, t, :], ident)
                mm.then_inc(done, 1)

            def project(xT, w, bank, done):
                for t in range(TT):
                    mm = pe.matmul(bank[:, t * C:(t + 1) * C], xT[:, t * P:(t + 1) * P], w,
                                   start=True, stop=True)
                mm.then_inc(done, 1)

            def by_head(bank, lhs, rhs, c0, done):
                order = [(s, 4 * s + p) for p in range(4) for s in range(2)]
                order += [(1 - s, 4 * s + p) for p in range(4) for s in range(2)]
                pe.sem_inc(S["heads_go"], 1)
                for s, q in order:
                    h = slice(s * NL, (s + 1) * NL)
                    mm = pe.matmul(pairs(bank)[h, q, c0:ZC], lhs[h, q, 0:NL], rhs[h, q, c0:ZC],
                                   start=True, stop=True)
                mm.then_inc(done, 1)

            def softmaxes(b, slot):
                if slot == 0:
                    pe.wait_ge(S["a_xn_ready"], b + 1)
                    if not isinstance(b, int) or b > 0:
                        pe.wait_ge(S["LT_act"], 2 * b)
                        pe.wait_ge(S["LT_dve"], 2 * b)
                    turn(a_xn, PS[:, 0, :], S["a_xT_ps"])
                if slot == 1:
                    pe.wait_ge(S["a_xT_ready"], b + 1)
                    project(a_xT, wqkv[:, 2 * C:3 * C], PS[:, 1, :], S["v_ps"])
                    for n in range(2):
                        mm = pe.matmul(PS[:, 0, n * T:(n + 1) * T], wqkv[:, n * C:(n + 1) * C], a_xT[:, :],
                                       start=True, stop=True)
                    mm.then_inc(S["qk_ps"], 1)
                if slot == 3:
                    pe.wait_ge(S["qz_ready"], b + 1)
                    for p in range(NP):
                        mm = pe.matmul(PS[:, 0, p * NL:(p + 1) * NL], qz[:, 2 * p:2 * p + 2, :], klu[:, :],
                                       start=True, stop=True)
                    mm.then_inc(S["K_ps"], 1)
                if slot in (4, 6):
                    h = (slot - 4) // 2
                    if h == 0:
                        pe.wait_ge(S["K_sub"], b + 1)
                    else:
                        pe.wait_ge(S["NT_act"], 2 * b + 1)
                        pe.wait_ge(S["NT_dve"], 2 * b + 1)
                    for p in range(4):
                        q = 8 * h + 2 * p
                        mm = pe.matmul(PS[:, p // 2, p % 2 * T:(p % 2 + 1) * T], qz[:, q:q + 2, :],
                                       qkT[:, 1, :], start=True, stop=True)
                    mm.then_inc(S["N_ps"], 1)
                if slot in (5, 7):
                    h = (slot - 5) // 2
                    pe.wait_ge(S["N_exp"], 2 * b + h + 1)
                    for t in range(TT):
                        for p in range(4):
                            mm = pe.transpose(PS[:, t, p * P:(p + 1) * P], EN[:, p, t * P:(t + 1) * P], ident)
                        mm.then_inc(S["NT_ps"], 1)
                if slot == 9:
                    pe.wait_ge(S["K_ready"], b + 1)
                    pe.wait_ge(S["NT_dve"], 2 * b + 2)
                    pe.matmul(PS[:, 1, :], const("halfsum"), Kw[:, :, 0:NL], start=True, stop=True
                              ).then_inc(S["cs_ps"], 1)
                    pe.wait_ge(S["NT_act"], 2 * b + 2)
                    for p in range(NP):
                        for t in range(TT):
                            to = min(p + WIDE, NP)
                            mm = pe.matmul(PS[:, 0, p * 2 * VC:to * 2 * VC], ENT[:, t, p, :],
                                           v1[:, t, 2 * p:2 * to, :], start=(t == 0), stop=(t == TT - 1))
                    mm.then_inc(S["nv_ps"], 1)
                if slot == 10:
                    pe.wait_ge(S["w_ready"], b + 1)
                    by_head(0, Kw, Kw, 0, S["Y0_ps"])
                if slot in (12, 14):
                    h = (slot - 12) // 2
                    if h == 0:
                        pe.wait_ge(S["YZ_ready"], b * NITER + 1)
                        pe.wait_ge(S["kz_ready"], b + 1)
                    else:
                        pe.wait_ge(S["LT_act"], 2 * b + 1)
                        pe.wait_ge(S["LT_dve"], 2 * b + 1)
                    for t in range(TT):
                        mm = pe.matmul(PS[:, t, :], qkT[:, 0, t * P:(t + 1) * P], kz[:, 8 * h:8 * h + 8, :],
                                       start=True, stop=True)
                    mm.then_inc(S["L_ps"], 1)
                if slot in (13, 15):
                    h = (slot - 13) // 2
                    pe.wait_ge(S["L_exp"], 2 * b + h + 1)
                    for t in range(TT):
                        for p in range(4):
                            mm = pe.transpose(PS[:, t, p * P:(p + 1) * P],
                                              EL[:, t, 2 * p:2 * p + 2, :], ident)
                        mm.then_inc(S["LT_ps"], 1)

            def inverse(b, slot):
                j, cube = slot // 2, slot % 2
                if j < NITER and not cube:
                    pe.wait_ge(S["YZ_ready"], b * NITER + j + 1)
                    if j == 0 and (not isinstance(b, int) or b > 0):
                        pe.wait_ge(S["x2_ready"], b)
                    by_head(2, Yz, Yz, 0, S["sq_ps"])
                if j < NITER and cube:
                    pe.wait_ge(S["M_ready"], b * NITER + j + 1)
                    by_head(2, Az, Mr, NL if j == NITER - 1 else 0, S["cube_ps"])
                if slot == 12:
                    pe.wait_ge(S["zp_ready"], b + 1)
                    pe.wait_ge(S["LT_act"], 2 * b + 2)
                    pe.wait_ge(S["LT_dve"], 2 * b + 2)
                    for t in range(TT):
                        for p in range(NP):
                            to = min(p + WIDE, NP)
                            mm = pe.matmul(PS[:, 2, (t * NP + p) * 2 * VC:(t * NP + to) * 2 * VC],
                                           ELT[:, t, p, :], zp[:, p:to, :], start=True, stop=True)
                    mm.then_inc(S["y_ps"], 1)
                if slot == 13:
                    pe.wait_ge(S["y_ready"], b + 1)
                    turn(yat[:, :, :, :].rearrange("p t h d -> p t (h d)"), PS[:, 3, :], S["yT_ps"])
                if slot == 14:
                    pe.wait_ge(S["yT_ready"], b + 1)
                    project(yT, wproj[:, :], PS[:, 2, :], S["proj_ps"])
                if slot == 16:
                    pe.wait_ge(S["f_xn_ready"], b + 1)
                    turn(f_xn, PS[:, 3, :], S["f_xT_ps"])
                if slot == 17:
                    pe.wait_ge(S["f_xT_ready"], b + 1)
                    project(f_xT, ffnM[:, :], PS[:, 2, :], S["f_ps"])

            def inner(b, slot):
                bank = PS[:, 4, :]
                if slot == 2:
                    pe.wait_ge(S["m_xn_ready"], b + 1)
                    turn(m_xn, bank, S["m_xT_ps"])
                if slot == 3:
                    pe.wait_ge(S["m_xT_ready"], b + 1)
                    for d in range(DT):
                        for k in range(KC):
                            mm = pe.matmul(bank[:, d * T:(d + 1) * T], wconv[:, k, d * P:(d + 1) * P],
                                           xpT[:, k:k + T], start=(k == 0), stop=(k == KC - 1))
                    mm.then_inc(S["conv_ps"], 1)
                if slot == 4:
                    pe.wait_ge(S["conv_out"], b + 1)
                    for d in range(DT):
                        mm = pe.matmul(bank[:, d * T:(d + 1) * T], win[:, DI + d * P:DI + (d + 1) * P],
                                       xpT[:, KC - 1:KC - 1 + T], start=True, stop=True)
                    mm.then_inc(S["res_ps"], 1)
                if slot == 9:
                    pe.wait_ge(S["res_out"], b + 1)
                    pe.wait_ge(S["u_ready"], b + 1)
                    for d in range(DT):
                        mm = pe.matmul(bank[0:RK, 0:T], wx[:, d, 0:RK], u[:, d, :],
                                       start=(d == 0), stop=(d == DT - 1))
                    mm.then_inc(S["dlr_ps"], 1)
                if slot == 11:
                    pe.wait_ge(S["dlr_ready"], b + 1)
                    for s in range(2):
                        for d in range(DT):
                            mm = pe.matmul(bank[0:3 * NS, s * T:(s + 1) * T], wx3[:, d, s, :, :], u[:, d, :],
                                           start=(d == 0), stop=(d == DT - 1))
                    mm.then_inc(S["bc_ps"], 1)
                if slot == 13:
                    pe.wait_ge(S["bc_hi"], b + 1)
                    for d in range(DT):
                        mm = pe.matmul(bank[:, d * T:(d + 1) * T], wdt[:, d * P:(d + 1) * P], dlr[:, :],
                                       start=True, stop=True)
                    mm.then_inc(S["dt_ps"], 1)

            def scans(b, slot):
                if slot in UNIT_AT:
                    k = UNIT_AT[slot]
                    if k == 0:
                        pe.wait_ge(S["bc_ready"], b + 1)
                        if not isinstance(b, int) or b > 0:
                            pe.wait_ge(S["x4_ready"], b)
                    else:
                        pe.wait_ge(S["c_ready"], b * NU + k)
                    for n in range(NQ):
                        mm = pe.matmul(PS[:, 6, n * T:(n + 1) * T], pick_s[:, NQ * k + n, :], bcs[:, 1, :],
                                       start=True, stop=True)
                    mm.then_inc(S["c_ps"], 1)
                    if k > 0:
                        pe.wait_ge(S["dBu_ready"], b * NU + k)
                    for n in range(NQ):
                        mm = pe.matmul(PS[:, 5, n * T:(n + 1) * T], pick_s[:, NQ * k + n, :], bcs[:, 0, :],
                                       start=True, stop=True)
                    mm.then_inc(S["b_ps"], 1)
                if slot == 13:
                    pe.wait_ge(S["ym_ready"], b + 1)
                    for t in range(TT):
                        for d in range(DT):
                            mm = pe.matmul(PS[:, 5, t * C:(t + 1) * C], ym[:, d, t * P:(t + 1) * P],
                                           wout[:, d, :], start=(d == 0), stop=(d == DT - 1))
                    mm.then_inc(S["out_ps"], 1)
                if slot == 15:
                    pe.wait_ge(S["g_xn_ready"], b + 1)
                    turn(g_xn, PS[:, 6, :], S["g_xT_ps"])
                if slot == 16:
                    pe.wait_ge(S["g_xT_ready"], b + 1)
                    project(g_xT, ffnM[:, :], PS[:, 5, :], S["g_ps"])

            pipeline(pe, (1, inverse), (3, scans), (2, inner), (0, softmaxes))

        @block.scalar
        def _(act):
            act.preload_act_table_set("natural_log_exp_and_others")

            def copy(dst, src, scale=1.0):
                return act.activation(dst, src, ACT.Copy, scale=scale)

            def first_rstd(b, n):
                act.wait_ge(var_ready[n], b + 1)
                act_link[n](act, act.activation(rs[n][:, 0, :], mv[n][:, :, 1], ACT.Ln, bias=const("eps")))
                act.activation(rs[n][:, 1, :], rs[n][:, 0, :], ACT.Exp, scale=-0.5).then_inc(rs0_ready[n], 1)

            act.wait_ge(S["weights_in"], 16 * NW)
            act.wait_ge(S["tables_in"], 16)
            act.wait_ge(S["filled"], 1)
            act.activation(negA[:, :, :], negA[:, :, :], ACT.Exp).then_inc(S["expA"], 1)
            act.wait_ge(S["expA"], 1)
            act.activation(negA[:, :, :], negA[:, :, :], ACT.Copy, scale=-1.0).then_inc(S["negA_ready"], 1)
            act.activation(pick_s[0:3 * NS, :, :], pick_f[:, :].rearrange("p (n m) -> p n m", m=P), ACT.Copy
                           ).then_inc(S["pick_cast"], 1)
            act.wait_ge(S["fT_ps"], 1)
            copy(fT[:, :, :], PS[:, 0, 0:2 * P].rearrange("p (a m) -> p a m", m=P)).then_inc(S["fT_sb"], 1)
            act.wait_ge(S["ffnM_ps"], 1)
            copy(ffnM[:, :], PS[:, 1, 0:P]).then_inc(S["ffnM_sb"], 1)
            act.wait_ge(S["negA_ready"], 1)
            act.wait_ge(S["zeros_ready"], 1)

            def prepare(b, slot):
                if slot == 15:
                    act_link[0].start(b)
                    first_rstd(b, 0)

            def softmaxes(b, slot):
                if slot == 0:
                    act.wait_ge(S["a_xT_ps"], b + 1)
                    copy(a_xT[:, :], PS[:, 0, 0:T]).then_inc(S["a_xT_ready"], 1)
                if slot == 1:
                    act.wait_ge(S["qk_ps"], b + 1)
                    copy(qkT[:, :, :], PS[:, 0, :].rearrange("p (a t) -> p a t", a=2)).then_inc(S["qk_ready"], 1)
                if slot == 3:
                    act.wait_ge(S["K_sub"], b + 1)
                    act.activation(Kw[:, :, 0:NL], Kw[:, :, 0:NL], ACT.Exp).then_inc(S["K_exp"], 1)
                if slot in (4, 6):
                    h = (slot - 4) // 2
                    act.wait_ge(S["N_max"], 2 * b + h + 1)
                    for p in range(4):
                        ins = act.activation(EN[:, p, :], PS[:, p // 2, p % 2 * T:(p % 2 + 1) * T], ACT.Exp,
                                             bias=nmaxN[:, 4 * h + p:4 * h + p + 1])
                    ins.then_inc(S["N_exp"], 1)
                if slot in (5, 7):
                    h = (slot - 5) // 2
                    act.wait_ge(S["NT_ps"], 4 * b + 2 * h + 1)
                    copy(ENT[:, 0, 4 * h:4 * h + 4, :], PS[:, 0, :].rearrange("p (q m) -> p q m", m=P)
                         ).then_inc(S["NT_act"], 1)
                if slot in (12, 14):
                    h = (slot - 12) // 2
                    act.wait_ge(S["L_sub"], 2 * b + h + 1)
                    act.activation(EL[:, :, :, :], EL[:, :, :, :], ACT.Exp).then_inc(S["L_exp"], 1)
                if slot in (13, 15):
                    h = (slot - 13) // 2
                    act.wait_ge(S["LT_ps"], 4 * b + 2 * h + 1)
                    copy(ELT[:, 0, 4 * h:4 * h + 4, :], PS[:, 0, :].rearrange("p (q m) -> p q m", m=P)
                         ).then_inc(S["LT_act"], 1)

            def inverse(b, slot):
                j, cube = slot // 2, slot % 2
                if slot == 0:
                    act_link[1].start(b)
                if j < NITER and not cube:
                    act.wait_ge(S["sq_ps"], b * NITER + j + 1)
                    copy(Az[:, :, :], pairs(2)[:, :, 0:ZC]).then_inc(S["A_ready"], 1)
                if slot == 13:
                    act.wait_ge(S["yT_ps"], b + 1)
                    copy(yT[:, :], PS[:, 3, 0:T]).then_inc(S["yT_ready"], 1)
                if slot == 14:
                    first_rstd(b, 1)
                if slot == 16:
                    act.wait_ge(S["f_xT_ps"], b + 1)
                    copy(f_xT[:, :], PS[:, 3, 0:T]).then_inc(S["f_xT_ready"], 1)

            def inner(b, slot):
                bank, link = PS[:, 4, :], act_link[2]
                if slot == 0:
                    link.start(b)
                    first_rstd(b, 2)
                if slot == 2:
                    act.wait_ge(S["m_xT_ps"], b + 1)
                    copy(xpT[:, KC - 1:KC - 1 + T], bank[:, 0:T]).then_inc(S["m_xT_ready"], 1)
                if slot == 3:
                    act.wait_ge(S["conv_ps"], b + 1)
                    for d in range(DT):
                        ins = act.activation(vr[:, 0, d, :], bank[:, d * T:(d + 1) * T], ACT.Identity,
                                             bias=convb[:, d:d + 1])
                    ins.then_inc(S["conv_out"], 1)
                if slot == 4:
                    act.wait_ge(S["res_ps"], b + 1)
                    copy(vr[:, 1, :, :], bank.rearrange("p (d t) -> p d t", t=T)).then_inc(S["res_out"], 1)
                    act.wait_ge(S["res_out"], b + 1)
                    act.activation(gate[:, :, :, :], vr[:, :, :, :], ACT.Exp, scale=-1.0
                                   ).then_inc(S["gate_exp"], 1)
                if slot == 6:
                    act.wait_ge(S["gate_cut"], b + 1)
                    link(act, act.activation(gate[:, :, :, :], gate[:, :, :, :], ACT.Ln, bias=const("one")))
                    act.activation(gate[:, :, :, :], gate[:, :, :, :], ACT.Exp, scale=-1.0
                                   ).then_inc(S["gate_ready"], 1)
                if slot == 9:
                    act.wait_ge(S["dlr_ps"], b + 1)
                    copy(dlr[:, :], bank[0:RK, 0:T]).then_inc(S["dlr_ready"], 1)
                if slot == 11:
                    act.wait_ge(S["bc_ps"], b + 1)
                    src = bank[0:3 * NS, :].rearrange("p (s t) -> p s t", t=T)
                    copy(bc[:, :, :], src)
                    copy(bch[:, :, :], src).then_inc(S["bc_hi"], 1)
                if slot == 13:
                    act.wait_ge(S["dt_ps"], b + 1)
                    for d in range(DT):
                        ins = act.activation(spa[:, d, :], bank[:, d * T:(d + 1) * T], ACT.Abs,
                                             bias=bdt[:, d:d + 1])
                    ins.then_inc(S["abs_read"], 1)
                if slot == 14:
                    act.wait_ge(S["abs_read"], b + 1)
                    link(act, act.activation(spa[:, :, :], spa[:, :, :], ACT.Exp, scale=-1.0))
                    act.activation(spa[:, :, :], spa[:, :, :], ACT.Ln, bias=const("one")
                                   ).then_inc(S["sp_ready"], 1)

            def copy_c(b, slot):
                if slot == 0:
                    act_link[3].start(b)
                if slot in UNIT_AT:
                    k = UNIT_AT[slot]
                    if k >= 2:
                        act.wait_ge(S["hs_ready"], b * NU + k - 1)
                    act.wait_ge(S["c_ps"], b * NU + k + 1)
                    copy(c_sb[:, k % 2, :, :], PS[:, 6, :].rearrange("p (n t) -> p n t", t=T)
                         ).then_inc(S["c_ready"], 1)
                if slot == 0:
                    decay(b, 0)
                if slot == 13:
                    first_rstd(b, 3)
                if slot == 15:
                    act.wait_ge(S["g_xT_ps"], b + 1)
                    copy(g_xT[:, :], PS[:, 6, 0:T]).then_inc(S["g_xT_ready"], 1)

            def decay(b, k):
                if k == 0:
                    act.wait_ge(S["delta_ready"], b + 1)
                if k >= 2:
                    act.wait_ge(S["h_ready"], b * NU + k - 1)
                for d in range(DT):
                    for n in range(NQ):
                        ins = act.activation(dA[:, k % 2, d, n, 1:T], delta[:, d, 1:T], ACT.Exp,
                                             scale=negA[:, d, NQ * k + n:NQ * k + n + 1])
                ins.then_inc(S["dA_ready"], 1)

            def decays(b, slot):
                if slot in UNIT_AT and UNIT_AT[slot] < NU - 1:
                    decay(b, UNIT_AT[slot] + 1)

            pipeline(act, (1, inverse), (3, copy_c), (-1, prepare), (0, softmaxes), (3, decays), (2, inner))

        @block.gpsimd
        def _(pool):
            pool.memset(pick_s[:, :, :], 0.0)
            pool.memset(bcs[:, :, :], 0.0)
            pool.memset(zp[:, :, :], 0.0)
            pool.memset(dA[:, :, :, :, :], 0.0)
            pool.memset(xpT[:, :], 0.0)
            pool.memset(v1[:, :, :, :], 1.0).then_inc(S["filled"], 1)
            pool.wait_ge(S["filled"], 1)
            pool.memset(zp[0:NL, :, HS], YS)
            pool.memset(zp[NL:P, :, VC + HS], YS).then_inc(S["zeros_ready"], 1)

            def biased(b, dst, src, ready, done):
                pool.wait_ge(ready, b + 1)
                pool.tensor_tensor(dst[:, :, :], src[:, :, :], bias_b[:, :].unsqueeze(1).broadcast_to([P, TT, C]),
                                   ALU.add).then_inc(done, 1)

            def softmaxes(b, slot):
                if slot == 3:
                    pool.wait_ge(S["lm_ready"], b + 1)
                    pool.tensor_tensor(kz[:, :, :], lm[:, 1, :].unsqueeze(1).broadcast_to([P, NH, NL]),
                                       const("headmask").unsqueeze(2).broadcast_to([P, NH, NL]), ALU.mult
                                       ).then_inc(S["kz_ready"], 1)

            def inverse(b, slot):
                if slot == 14:
                    biased(b, x1b, x1, S["x1_ready"], S["x1b_ready"])

            def inner(b, slot):
                if slot == 7:
                    pool.wait_ge(S["gate_ready"], b + 1)
                    pool.tensor_tensor(u[:, :, :], vr[:, 0, :, :], gate[:, 0, :, :], ALU.mult
                                       ).then_inc(S["u_ready"], 1)
                if slot == 15:
                    pool.wait_ge(S["sp_ready"], b + 1)
                    pool.wait_ge(S["max_ready"], b + 1)
                    pool.tensor_tensor(delta[:, :, :], spp[:, :, :], spa[:, :, :], ALU.add
                                       ).then_inc(S["delta_ready"], 1)
                    pool.wait_ge(S["delta_ready"], b + 1)
                    pool.tensor_tensor(du[:, :, :], delta[:, :, :], u[:, :, :], ALU.mult
                                       ).then_inc(S["du_ready"], 1)
                if slot == 16:
                    if not isinstance(b, int) or b > 0:
                        pool.wait_ge(S["ym_ready"], b)
                    pool.tensor_tensor(sres[:, :, :], vr[:, 1, :, :], gate[:, 1, :, :], ALU.mult
                                       ).then_inc(S["sres_ready"], 1)

            def scans(b, slot):
                if slot in UNIT_AT:
                    k = UNIT_AT[slot]
                    pool.wait_ge(S["h_ready"], b * NU + k + 1)
                    pool.wait_ge(S["c_ready"], b * NU + k + 1)
                    pool.tensor_tensor(hc[:, :, :, :].rearrange("p d n t -> p d (n t)"),
                                       hst[:, k % 2, :, :, :].rearrange("p d n t -> p d (n t)"),
                                       c_sb[:, k % 2, :, :].rearrange("p n t -> p (n t)").unsqueeze(1)
                                       .broadcast_to([P, DT, NQ * T]), ALU.mult).then_inc(S["hc_ready"], 1)
                    pool.wait_ge(S["hc_ready"], b * NU + k + 1)
                    if k >= 2:
                        pool.wait_ge(S["y_acc"], b * NU + k - 1)
                    pool.tensor_tensor(hs[:, k % 2, :, :], hc[:, :, 0, :], hc[:, :, 1, :], ALU.add
                                       ).then_inc(S["hs_ready"], 1)
                    pool.wait_ge(S["hs_ready"], b * NU + k + 1)
                if slot == 13:
                    biased(b, x3b, x3, S["x3_ready"], S["x3b_ready"])

            pool.wait_ge(S["weights_in"], 16 * NW)
            pool.wait_ge(S["tables_in"], 16)
            pipeline(pool, (1, inverse), (3, scans), (2, inner), (0, softmaxes))

        @block.vector
        def _(dve):
            dve.wait_ge(S["weights_in"], 16 * NW)
            dve.wait_ge(S["tables_in"], 16)
            dve.tensor_tensor(wconv[:, :, :], convw_b[:, :, :],
                              win[:, 0:DI].unsqueeze(1).broadcast_to([P, KC, DI]), ALU.mult
                              ).then_inc(S["convw_ready"], 1)
            for s in range(2):
                for r in range(3):
                    ins = dve.tensor_copy(wx3[:, :, s, r, :], wx[:, :, RK + s * NS:RK + (s + 1) * NS])
            ins.then_inc(S["wx3_ready"], 1)
            dve.wait_ge(S["zeros_ready"], 1)

            def statistics(n, src):
                for t in range(TT):
                    ins = dve.bn_stats(st[n][:, t, :], src[:, t, :])
                dve_link[n](dve, ins)
                dve.memset(pause[:, :], 0.0)
                for t in range(TT):
                    ins = dve.bn_aggr(mv[n][:, t, :], st[n][:, t, :])
                ins.then_inc(var_ready[n], 1)

            def normalise(b, n, src, dst, done):
                link, r = dve_link[n], rs[n]
                dve.wait_ge(rs0_ready[n], b + 1)
                link(dve, dve.tensor_tensor(r[:, 2, :], r[:, 1, :], r[:, 1, :], ALU.mult))
                link(dve, dve.scalar_tensor_tensor(out=r[:, 3, :], in0=mv[n][:, :, 1], scalar=EPS,
                                                   in1=r[:, 2, :], op0=ALU.add, op1=ALU.mult))
                link(dve, dve.tensor_scalar(r[:, 2, :], r[:, 3, :], -0.5, 1.5, ALU.mult, ALU.add))
                link(dve, dve.tensor_tensor(r[:, 3, :], r[:, 2, :], r[:, 1, :], ALU.mult))
                for t in range(TT):
                    ins = dve.tensor_scalar(dst[:, t, :], src[:, t, :], mv[n][:, t, 0:1], r[:, 3, t:t + 1],
                                            ALU.subtract, ALU.mult)
                ins.then_inc(done, 1)

            def spread(ap, n):
                return ap.unsqueeze(2).broadcast_to([ap.shape[0], ap.shape[1], n])

            def add_rows(dst, src, bank, done):
                dve.tensor_tensor(dst[:, :, :], src[:, :, :], bank[:, 0:T].rearrange("p (t c) -> p t c", c=C),
                                  ALU.add).then_inc(done, 1)

            def prepare(b, slot):
                if slot == 15:
                    dve_link[0].start(b)
                    dve.wait_ge(S["x_in"], 16 * b + 16)
                    statistics(0, xin)
                if slot == 16:
                    if not isinstance(b, int) or b > 0:
                        dve.wait_ge(S["a_xT_ps"], b)
                    normalise(b, 0, xin, a_xn, S["a_xn_ready"])

            def softmaxes(b, slot):
                link = dve_link[4]
                if slot == 0:
                    link.start(b)
                if slot == 1:
                    dve.wait_ge(S["v_ps"], b + 1)
                    dve.tensor_copy(v1[:, :, :, 0:HS].rearrange("p t h d -> p (t h) d"),
                                    PS[:, 1, 0:T].rearrange("p (t d) -> p t d", d=HS)
                                    ).then_inc(S["v_ready"], 1)
                if slot == 2:
                    dve.wait_ge(S["qk_ready"], b + 1)
                    dve.tensor_reduce(lm[:, :, :].rearrange("p a l -> p (a l)"),
                                      qkT[:, :, :].rearrange("p a (l r) -> p (a l) r", r=POOLED),
                                      AX.X, ALU.add).then_inc(S["lm_ready"], 1)
                    dve.wait_ge(S["lm_ready"], b + 1)
                    dve.tensor_scalar(klu[:, :], lm[:, 1, :], 1.0 / POOLED, None, ALU.mult)
                    dve.tensor_tensor(qz[:, :, :], lm[:, 0, :].unsqueeze(1).broadcast_to([P, NH, NL]),
                                      spread(const("headmask"), NL), ALU.mult).then_inc(S["qz_ready"], 1)
                if slot == 3:
                    dve.wait_ge(S["K_ps"], b + 1)
                    sc = PS[:, 0, :].rearrange("p (q m) -> p q m", m=NL)
                    link(dve, dve.tensor_reduce(nmaxK[:, :], sc, AX.X, ALU.max, negate=True))
                    dve.tensor_tensor(Kw[:, :, 0:NL], sc, spread(nmaxK[:, :], NL), ALU.add
                                      ).then_inc(S["K_sub"], 1)
                if slot in (4, 6):
                    h = (slot - 4) // 2
                    dve.wait_ge(S["N_ps"], 2 * b + h + 1)
                    dve.tensor_reduce(nmaxN[:, 4 * h:4 * h + 4],
                                      PS[:, 0:2, :].rearrange("p g (j t) -> p (g j) t", t=T),
                                      AX.X, ALU.max, negate=True).then_inc(S["N_max"], 1)
                if slot == 4:
                    dve.wait_ge(S["K_exp"], b + 1)
                    link(dve, dve.tensor_reduce(sumK[:, :], Kw[:, :, 0:NL], AX.X, ALU.add))
                    link(dve, dve.reciprocal(rsumK[:, :], sumK[:, :]))
                    dve.tensor_tensor(Kw[:, :, 0:NL], Kw[:, :, 0:NL], spread(rsumK[:, :], NL), ALU.mult
                                      ).then_inc(S["K_ready"], 1)
                if slot in (5, 7):
                    h = (slot - 5) // 2
                    dve.wait_ge(S["NT_ps"], 4 * b + 2 * h + 2)
                    dve.tensor_copy(ENT[:, 1, 4 * h:4 * h + 4, :], PS[:, 1, :].rearrange("p (q m) -> p q m", m=P)
                                    ).then_inc(S["NT_dve"], 1)
                if slot == 9:
                    dve.wait_ge(S["cs_ps"], b + 1)
                    link(dve, dve.tensor_reduce(den[:, :], PS[:, 1, :].rearrange("p (q m) -> p q m", m=NL),
                                                AX.X, ALU.max))
                    dve.reciprocal(rden[:, :], den[:, :])
                    dve.wait_ge(S["nv_ps"], b + 1)
                    nv = PS[:, 0, 0:NP * 2 * VC].rearrange("p (q c) -> p q c", c=2 * VC)
                    for s in range(2):
                        h = slice(s * NL, (s + 1) * NL)
                        ins = dve.reciprocal(rsumN[h, :], nv[h, :, s * VC + HS])
                    link(dve, ins)
                    for s in range(2):
                        h = slice(s * NL, (s + 1) * NL)
                        ins = dve.tensor_tensor(Kw[h, :, NL:ZC], nv[h, :, s * VC:s * VC + HS],
                                                spread(rsumN[h, :], HS), ALU.mult)
                    ins.then_inc(S["w_ready"], 1)
                if slot == 10:
                    dve.wait_ge(S["Y0_ps"], b + 1)
                    if not isinstance(b, int) or b > 0:
                        dve.wait_ge(S["H_ready"], b * NITER)
                    dve.tensor_tensor(Yz[:, :, :], pairs(0)[:, :, 0:ZC], spread(rden[:, :], ZC), ALU.mult
                                      ).then_inc(S["YZ_ready"], 1)
                if slot in (12, 14):
                    h = (slot - 12) // 2
                    dve.wait_ge(S["L_ps"], 2 * b + h + 1)
                    flat = PS[:, 0:2, :].rearrange("p a (j m) -> p (a j) m", m=NL)
                    link(dve, dve.tensor_reduce(nmaxL[:, :], flat, AX.X, ALU.max, negate=True))
                    dve.tensor_tensor(EL[:, :, :, :].rearrange("p t j m -> p (t j) m"), flat,
                                      spread(nmaxL[:, :], NL), ALU.add).then_inc(S["L_sub"], 1)
                if slot in (13, 15):
                    h = (slot - 13) // 2
                    dve.wait_ge(S["LT_ps"], 4 * b + 2 * h + 2)
                    dve.tensor_copy(ELT[:, 1, 4 * h:4 * h + 4, :], PS[:, 1, :].rearrange("p (q m) -> p q m", m=P)
                                    ).then_inc(S["LT_dve"], 1)

            def inverse(b, slot):
                j, cube, last = slot // 2, slot % 2, slot // 2 == NITER - 1
                c0 = NL if last else 0
                if slot == 0:
                    dve_link[1].start(b)
                    dve.wait_ge(S["YZ_ready"], b * NITER + 1)
                if j < NITER and not cube:
                    dve.wait_ge(S["A_ready"], b * NITER + j + 1)
                    if j > 0:
                        dve.wait_ge(S["YZ_ready"], b * NITER + j + 1)
                    for dst, part, ready in ((Mr, -1.0 / 7.0, "M_ready"), (Hz, -15.0 / 13.0, "H_ready")):
                        dve.scalar_tensor_tensor(out=dst[:, :, c0:ZC], in0=Az[:, :, c0:ZC], scalar=part / YS,
                                                 in1=Yz[:, :, c0:ZC], op0=ALU.mult, op1=ALU.add
                                                 ).then_inc(S[ready], 1)
                if j < NITER and cube:
                    dve.wait_ge(S["cube_ps"], b * NITER + j + 1)
                    dve.wait_ge(S["H_ready"], b * NITER + j + 1)
                    if last:
                        for s in range(2):
                            h = slice(s * NL, (s + 1) * NL)
                            ins = dve.scalar_tensor_tensor(out=zp[h, :, s * VC:s * VC + HS],
                                                           in0=Hz[h, :, NL:ZC], scalar=3.25,
                                                           in1=pairs(2)[h, :, NL:ZC], op0=ALU.mult, op1=ALU.add)
                        ins.then_inc(S["zp_ready"], 1)
                    else:
                        dve.scalar_tensor_tensor(out=Yz[:, :, :], in0=Hz[:, :, :], scalar=3.25,
                                                 in1=pairs(2)[:, :, 0:ZC], op0=ALU.mult, op1=ALU.add
                                                 ).then_inc(S["YZ_ready"], 1)
                if slot == 12:
                    dve.wait_ge(S["y_ps"], b + 1)
                    yp = PS[:, 2, 0:TT * NH * VC].rearrange("p (t c) -> p t c", c=VC)
                    dve_link[1](dve, dve.reciprocal(rsumL[:, :], yp[:, :, HS]))
                    dve.tensor_tensor(yat[:, :, :, :].rearrange("p t h d -> p (t h) d"), yp[:, :, 0:HS],
                                      spread(rsumL[:, :], HS), ALU.mult).then_inc(S["y_ready"], 1)
                if slot == 14:
                    dve.wait_ge(S["proj_ps"], b + 1)
                    dve.wait_ge(S["xres_in"], 16 * b + 16)
                    add_rows(x1, xres, PS[:, 2, :], S["x1_ready"])
                    dve.wait_ge(S["x1_ready"], b + 1)
                    statistics(1, x1)
                if slot == 15:
                    normalise(b, 1, x1, f_xn, S["f_xn_ready"])
                if slot == 17:
                    dve.wait_ge(S["f_ps"], b + 1)
                    dve.wait_ge(S["x1b_ready"], b + 1)
                    add_rows(x2, x1b, PS[:, 2, :], S["x2_ready"])

            def inner(b, slot):
                bank, link = PS[:, 4, :], dve_link[2]
                if slot == 0:
                    link.start(b)
                    dve.wait_ge(S["x2_ready"], b + 1)
                    statistics(2, x2)
                if slot == 1:
                    normalise(b, 2, x2, m_xn, S["m_xn_ready"])
                if slot == 5:
                    dve.wait_ge(S["gate_exp"], b + 1)
                    dve.tensor_scalar(gate[:, :, :, :], gate[:, :, :, :], LN_MOST, None, ALU.min
                                      ).then_inc(S["gate_cut"], 1)
                if slot == 12:
                    dve.wait_ge(S["bc_hi"], b + 1)
                    link(dve, dve.scalar_tensor_tensor(out=bc[:, :, :], in0=bch[:, :, :],
                                                       scalar=const("part1")[0:3 * NS, :], in1=bc[:, :, :],
                                                       op0=ALU.mult, op1=ALU.add))
                    link(dve, dve.tensor_copy(bch[:, :, :], bc[:, :, :]))
                if slot == 14:
                    dve.wait_ge(S["abs_read"], b + 1)
                    for d in range(DT):
                        ins = dve.tensor_scalar(spp[:, d, :], bank[:, d * T:(d + 1) * T], bdt[:, d:d + 1], 0.0,
                                                ALU.add, ALU.max)
                    ins.then_inc(S["max_ready"], 1)
                if slot == 15:
                    dve.scalar_tensor_tensor(out=bcs[0:3 * NS, :, :], in0=bch[:, :, :],
                                             scalar=const("part2")[0:3 * NS, :], in1=bc[:, :, :],
                                             op0=ALU.mult, op1=ALU.add).then_inc(S["bc_ready"], 1)
                if slot == 15:
                    if not isinstance(b, int) or b > 0:
                        dve.wait_ge(S["ym_ready"], b)
                    for d in range(DT):
                        ins = dve.tensor_scalar(uD[:, d, :], u[:, d, :], dskip[:, d:d + 1], None, ALU.mult)
                    ins.then_inc(S["uD_ready"], 1)
                if slot == 15:
                    if not isinstance(b, int) or b > 0:
                        dve.wait_ge(S["x3_ready"], b)
                    dve.tensor_copy(x2b[:, :, :], x2[:, :, :]).then_inc(S["x2b_ready"], 1)
                    dve.wait_ge(S["x2b_ready"], b + 1)

            def scans(b, slot):
                link = dve_link[3]
                if slot == 0:
                    link.start(b)
                    dve.wait_ge(S["du_ready"], b + 1)
                if slot in UNIT_AT:
                    k = UNIT_AT[slot]
                    dve.wait_ge(S["b_ps"], b * NU + k + 1)
                    if k >= 2:
                        dve.wait_ge(S["h_ready"], b * NU + k - 1)
                    dve.tensor_tensor(dBu[:, k % 2, :, :, :],
                                      PS[:, 5, :].rearrange("p (n t) -> p n t", t=T).unsqueeze(1)
                                      .broadcast_to([P, DT, NQ, T]),
                                      du[:, :, :].unsqueeze(2).broadcast_to([P, DT, NQ, T]), ALU.mult
                                      ).then_inc(S["dBu_ready"], 1)
                    dve.wait_ge(S["dBu_ready"], b * NU + k + 1)
                    dve.wait_ge(S["dA_ready"], b * NU + k + 1)
                    if k >= 2:
                        dve.wait_ge(S["hs_ready"], b * NU + k - 1)
                    dve.tensor_tensor_scan(hst[:, k % 2, :, :, :].rearrange("p d n t -> p (d n t)"),
                                           dA[:, k % 2, :, :, :].rearrange("p d n t -> p (d n t)"),
                                           dBu[:, k % 2, :, :, :].rearrange("p d n t -> p (d n t)"),
                                           0.0, ALU.mult, ALU.add).then_inc(S["h_ready"], 1)
                if slot == 12:
                    dve.wait_ge(S["y_acc"], b * NU + NU)
                    dve.wait_ge(S["sres_ready"], b + 1)
                    dve.tensor_tensor(ym[:, :, :], ysum[:, :, :], sres[:, :, :], ALU.mult
                                      ).then_inc(S["ym_ready"], 1)
                if slot == 13:
                    dve.wait_ge(S["out_ps"], b + 1)
                    add_rows(x3, x2b, PS[:, 5, :], S["x3_ready"])
                    dve.wait_ge(S["x3_ready"], b + 1)
                    statistics(3, x3)
                if slot == 14:
                    normalise(b, 3, x3, g_xn, S["g_xn_ready"])
                if slot == 16:
                    dve.wait_ge(S["g_ps"], b + 1)
                    dve.wait_ge(S["x3b_ready"], b + 1)
                    if isinstance(b, int) and b > 0:
                        dve.wait_ge(S["x_out"], 16 * b)
                    add_rows(x4, x3b, PS[:, 5, :], S["x4_ready"])

            def sums(b, slot):
                k = NU - 1 if slot == 11 else UNIT_AT.get(slot, 0) - 1
                if k >= 0:
                    dve.wait_ge(S["hs_ready"], b * NU + k + 1)
                    if k == 0:
                        dve.wait_ge(S["uD_ready"], b + 1)
                    else:
                        dve.wait_ge(S["y_acc"], b * NU + k)
                    dve.tensor_tensor(ysum[:, :, :], uD[:, :, :] if k == 0 else ysum[:, :, :],
                                      hs[:, k % 2, :, :], ALU.add).then_inc(S["y_acc"], 1)

            pipeline(dve, (1, inverse), (3, scans), (3, sums), (-1, prepare), (0, softmaxes), (2, inner))
            assert [l.n for l in dve_link] == list(DVE_LINKS)


_INS = ['L0_attn_a_x', 'L0_attn_a_W_attn', 'L0_attn_a_W_proj', 'L0_attn_b_W_in', 'L0_attn_b_conv_w',
        'L0_attn_b_conv_b', 'L0_attn_b_W_x', 'L0_attn_b_W_dt', 'L0_attn_b_b_dt', 'L0_attn_b_A_log',
        'L0_attn_b_D', 'L0_attn_b_W_out', 'L0_ffn_w_freq_real', 'L0_ffn_w_freq_imag', 'L0_ffn_bias']


def kernel(**inputs):
    import numpy as _np
    import concourse.bacc as _bacc
    from concourse import mybir as _mybir
    from concourse.bass_utils import run_bass_kernel_spmd as _run

    nc = _bacc.Bacc("TRN2", target_bir_lowering=False, num_devices=1)
    tab, pick = shape_tables()
    arrays, args = {}, []
    for name, a in [(n, inputs[n]) for n in _INS] + [("tab", tab), ("pick", pick)]:
        a = _np.ascontiguousarray(a)
        arrays[f"in_{name}"] = a
        args.append(nc.dram_tensor(f"in_{name}", a.shape, _mybir.dt.from_np(a.dtype), kind="ExternalInput").ap())
    args.append(nc.dram_tensor("out_x", (B, T, C), F32, kind="ExternalOutput").ap())
    hybrid_layer_kernel(nc, *args)
    r = _run(nc, [arrays], core_ids=[0])
    return r.results[0]["out_x"]
```
